# Optimizing a Trainium2 kernel written in Bass

```python
import numpy as np
import jax
import jax.numpy as jnp

def _softmax(x, axis=-1):
    return jax.nn.softmax(x, axis=axis)

def _gelu(x):
    return jax.nn.gelu(x, approximate=True)

def _silu(x):
    return jax.nn.silu(x)

def _sigmoid(x):
    return jax.nn.sigmoid(x)

def _layernorm(x, axis=-1, eps=1e-05):
    m = jnp.mean(x, axis=axis, keepdims=True)
    v = jnp.var(x, axis=axis, keepdims=True)
    return (x - m) / jnp.sqrt(v + eps)

def _scatter_add(tgt, idx, src, axis=0):
    return tgt.at[idx].add(src)

def _segment_sum(src, seg, n):
    return jax.ops.segment_sum(src, seg, n)
kernel_name = 'mk_decoder_preln_d1_seqx_r4_053203'

def setup_inputs(seed: int=0):
    np.random.seed(seed)
    _w = jnp.asarray

    def _rec_inputs():
        import jax
        import jax.numpy as jnp
        _rk = jax.random.key(seed)
        x = -0.0002928 + 1 * jax.random.normal(jax.random.fold_in(_rk, 1), (4, 1024, 256), jnp.float32)
        _lenS = 1024 - jax.random.randint(jax.random.fold_in(_rk, 7), (4,), 0, max(1, 1024 // 4) + 1, jnp.int32)
        _lenS2 = 64 - jax.random.randint(jax.random.fold_in(_rk, 8), (4,), 0, max(1, 64 // 4) + 1, jnp.int32)
        _ctx_1024P = jax.random.normal(jax.random.fold_in(_rk, 11), (4, 16, 256), jnp.float32)
        _ctx_1024c = jax.random.dirichlet(jax.random.fold_in(_rk, 511), 0.3 * jnp.ones((16,), jnp.float32), (4, 64))
        _ctx_1024t = jnp.einsum('bsk,bkd->bsd', _ctx_1024c, _ctx_1024P)
        _ctx_1024t = _ctx_1024t * jax.lax.rsqrt(jnp.mean(jnp.square(_ctx_1024t)) + 1e-12) * 0.953939
        ctx_1024 = -1.39393e-06 + 0.999914 * (_ctx_1024t + 0.3 * jax.random.normal(jax.random.fold_in(_rk, 611), (4, 64, 256), jnp.float32))
        _validS = jnp.arange(1024)[None, :] < _lenS[:, None]
        _validS2 = jnp.arange(64)[None, :] < _lenS2[:, None]
        _causal = jnp.tril(jnp.ones((1024, 1024), dtype=bool))
        mask_BxS2_bf0 = jnp.logical_not(jnp.ones((4, 64), dtype=bool))
        return (x, ctx_1024, mask_BxS2_bf0)
    x, ctx_1024, mask_BxS2_bf0 = _rec_inputs()

    def _L0_attn_setup():
        import jax, jax.numpy as jnp
        import numpy as np
        NUM_HEADS = 16
        NUM_KV_HEADS = 4
        HEAD_DIM = 64
        HIDDEN = 256
        R_SOFTPLUS_0 = 1.442695041
        key = jax.random.key(seed)
        ks = jax.random.split(key, 6)
        B, S = (2, 512)
        qkv_out = (NUM_HEADS + 2 * NUM_KV_HEADS) * HEAD_DIM
        return {'hidden_states': jax.random.normal(ks[0], (B, S, HIDDEN), dtype=jnp.float32), 'scaling': jax.random.normal(ks[1], (HEAD_DIM,), dtype=jnp.float32), 'qkv_w': jax.random.normal(ks[2], (qkv_out, HIDDEN), dtype=jnp.float32) * (1.0 / np.sqrt(HIDDEN)), 'qkv_b': jax.random.normal(ks[3], (qkv_out,), dtype=jnp.float32) * 0.01, 'o_w': jax.random.normal(ks[4], (HIDDEN, NUM_HEADS * HEAD_DIM), dtype=jnp.float32) * (1.0 / np.sqrt(NUM_HEADS * HEAD_DIM)), 'o_b': jax.random.normal(ks[5], (HIDDEN,), dtype=jnp.float32) * 0.01}
    _L0_attn_all = _L0_attn_setup()
    _L0_attn_in = {k: v for k, v in _L0_attn_all.items() if k in ('scaling', 'qkv_w', 'qkv_b', 'o_w', 'o_b')}
    del _L0_attn_all

    def _L0_xattn_setup():
        import jax, jax.numpy as jnp
        import numpy as np
        B, SQ, SKV, D, H = (2, 512, 512, 256, 16)
        HD = D // H

        def cross_attention(query, context, mask, Wq, bq, Wkv, bkv, Wout, bout, num_heads):
            b, sq, d = query.shape
            skv = context.shape[1]
            hd = d // num_heads
            scale = hd ** (-0.5)
            q = query @ Wq + bq
            kv = context @ Wkv + bkv
            kv = kv.reshape(b, skv, 2, num_heads, hd).transpose(2, 0, 3, 1, 4)
            k, v = (kv[0], kv[1])
            q = q.reshape(b, sq, num_heads, hd).transpose(0, 2, 1, 3)
            scores = jnp.einsum('bhid,bhjd->bhij', q, k) * scale
            scores = jnp.where(mask[:, None, None, :], -jnp.inf, scores)
            attn = jax.nn.softmax(scores, axis=-1)
            out = jnp.einsum('bhij,bhjd->bhid', attn, v)
            out = out.transpose(0, 2, 1, 3).reshape(b, sq, d)
            return out @ Wout + bout
        key = jax.random.key(seed)
        ks = jax.random.split(key, 6)
        scale = 1.0 / np.sqrt(D)
        return {'query': jax.random.normal(ks[0], (B, SQ, D), dtype=jnp.float32), 'context': jax.random.normal(ks[1], (B, SKV, D), dtype=jnp.float32), 'mask': jnp.zeros((B, SKV), dtype=bool), 'Wq': jax.random.normal(ks[2], (D, D), dtype=jnp.float32) * scale, 'bq': jnp.zeros((D,), dtype=jnp.float32), 'Wkv': jax.random.normal(ks[3], (D, 2 * D), dtype=jnp.float32) * scale, 'bkv': jnp.zeros((2 * D,), dtype=jnp.float32), 'Wout': jax.random.normal(ks[4], (D, D), dtype=jnp.float32) * scale, 'bout': jnp.zeros((D,), dtype=jnp.float32), 'num_heads': H}
    _L0_xattn_all = _L0_xattn_setup()
    _L0_xattn_in = {k: v for k, v in _L0_xattn_all.items() if k in ('Wq', 'bq', 'Wkv', 'bkv', 'Wout', 'bout')}
    del _L0_xattn_all

    def _L0_ffn_setup():
        import jax, jax.numpy as jnp
        import numpy as np
        D_MODEL = 256
        NUM_TILES = 64
        TPC = 8
        NUM_CLUSTERS = NUM_TILES // TPC
        GRID = 16
        COMP_H = 64
        NUM_KNOTS = 8
        EPS_LN = 1e-05

        def _calibrate(scores, knots, temperature):
            K = knots.shape[0]
            normalized = jax.nn.sigmoid(scores / (temperature[0] + 1e-06))
            idx_float = normalized * (K - 1)
            idx_low = jnp.clip(idx_float.astype(jnp.int32), 0, K - 2)
            idx_high = idx_low + 1
            t = idx_float - idx_low.astype(scores.dtype)
            val_low = knots[idx_low]
            val_high = knots[idx_high]
            return val_low + t * (val_high - val_low)

        def _forward(x, signatures_raw, knot_values, temperature, compress_w1, compress_b1, compress_w2, compress_b2, spline_w1, spline_b1, spline_w2, spline_b2, directions, norm_gamma, norm_beta, output_scale):
            B, T, D = x.shape
            xf = x.reshape(-1, D)
            q = jnp.where(signatures_raw > 0.3, 1.0, jnp.where(signatures_raw < -0.3, -1.0, 0.0)).astype(signatures_raw.dtype)
            sigs = signatures_raw + jax.lax.stop_gradient(q - signatures_raw)
            cluster_sigs = jnp.sign(sigs.reshape(NUM_CLUSTERS, TPC, D).mean(axis=1))
            cluster_scores = xf @ cluster_sigs.T
            cluster_gates = _calibrate(cluster_scores, knot_values, temperature)
            cluster_idx = jnp.argmax(cluster_gates, axis=-1)
            tile_scores = xf @ sigs.T
            tile_gates = _calibrate(tile_scores, knot_values, temperature)
            gates_by_cluster = tile_gates.reshape(-1, NUM_CLUSTERS, TPC)
            sel_gates = jnp.take_along_axis(gates_by_cluster, cluster_idx[:, None, None], axis=1)[:, 0, :]
            local_idx = jnp.argmax(sel_gates, axis=-1)
            tile_idx = cluster_idx * TPC + local_idx
            h = jax.nn.gelu(xf @ compress_w1 + compress_b1, approximate=False)
            comp = jnp.tanh(h @ compress_w2 + compress_b2)
            w1 = spline_w1[tile_idx]
            b1 = spline_b1[tile_idx]
            hh = jax.nn.relu(jnp.einsum('ni,nig->ng', comp, w1) + b1)
            w2 = spline_w2[tile_idx]
            b2 = spline_b2[tile_idx]
            mag = jnp.einsum('ng,ngo->no', hh, w2) + b2
            ffn_out = mag * directions[tile_idx] * output_scale[0]
            y = xf + ffn_out
            mu = y.mean(axis=-1, keepdims=True)
            var = ((y - mu) ** 2).mean(axis=-1, keepdims=True)
            y = (y - mu) / jnp.sqrt(var + EPS_LN) * norm_gamma + norm_beta
            return y.reshape(B, T, D)
        key = jax.random.key(seed)
        ks = jax.random.split(key, 12)
        B, T = (4, 1024)
        x = jax.random.normal(ks[0], (B, T, D_MODEL), dtype=jnp.float32)
        signatures_raw = jax.random.normal(ks[1], (NUM_TILES, D_MODEL), dtype=jnp.float32) * 0.5
        knot_values = jax.nn.sigmoid(jnp.linspace(-3.0, 3.0, NUM_KNOTS).astype(jnp.float32))
        temperature = jnp.ones((1,), dtype=jnp.float32)
        compress_w1 = jax.random.normal(ks[2], (D_MODEL, COMP_H), dtype=jnp.float32) * (1.0 / np.sqrt(D_MODEL))
        compress_b1 = jnp.zeros((COMP_H,), dtype=jnp.float32)
        compress_w2 = jax.random.normal(ks[3], (COMP_H, 2), dtype=jnp.float32) * (1.0 / np.sqrt(COMP_H))
        compress_b2 = jnp.zeros((2,), dtype=jnp.float32)
        spline_w1 = jax.random.normal(ks[4], (NUM_TILES, 2, GRID), dtype=jnp.float32) * (1.0 / np.sqrt(2.0))
        spline_b1 = jnp.zeros((NUM_TILES, GRID), dtype=jnp.float32)
        spline_w2 = jax.random.normal(ks[5], (NUM_TILES, GRID, 1), dtype=jnp.float32) * (1.0 / np.sqrt(GRID))
        spline_b2 = jnp.zeros((NUM_TILES, 1), dtype=jnp.float32)
        directions = jax.random.normal(ks[6], (NUM_TILES, D_MODEL), dtype=jnp.float32) * 0.02
        norm_gamma = jnp.ones((D_MODEL,), dtype=jnp.float32)
        norm_beta = jnp.zeros((D_MODEL,), dtype=jnp.float32)
        output_scale = jnp.ones((1,), dtype=jnp.float32) * 0.1
        return dict(x=x, signatures_raw=signatures_raw, knot_values=knot_values, temperature=temperature, compress_w1=compress_w1, compress_b1=compress_b1, compress_w2=compress_w2, compress_b2=compress_b2, spline_w1=spline_w1, spline_b1=spline_b1, spline_w2=spline_w2, spline_b2=spline_b2, directions=directions, norm_gamma=norm_gamma, norm_beta=norm_beta, output_scale=output_scale)
    _L0_ffn_all = _L0_ffn_setup()
    _L0_ffn_in = {k: v for k, v in _L0_ffn_all.items() if k in ('signatures_raw', 'knot_values', 'temperature', 'compress_w1', 'compress_b1', 'compress_w2', 'compress_b2', 'spline_w1', 'spline_b1', 'spline_w2', 'spline_b2', 'directions', 'norm_gamma', 'norm_beta', 'output_scale')}
    del _L0_ffn_all
    return {'x': x, 'ctx_1024': ctx_1024, 'mask_BxS2_bf0': mask_BxS2_bf0, 'L0_attn_scaling': _L0_attn_in['scaling'], 'L0_attn_qkv_w': _L0_attn_in['qkv_w'], 'L0_attn_qkv_b': _L0_attn_in['qkv_b'], 'L0_attn_o_w': _L0_attn_in['o_w'], 'L0_attn_o_b': _L0_attn_in['o_b'], 'L0_xattn_Wq': _L0_xattn_in['Wq'], 'L0_xattn_bq': _L0_xattn_in['bq'], 'L0_xattn_Wkv': _L0_xattn_in['Wkv'], 'L0_xattn_bkv': _L0_xattn_in['bkv'], 'L0_xattn_Wout': _L0_xattn_in['Wout'], 'L0_xattn_bout': _L0_xattn_in['bout'], 'L0_ffn_signatures_raw': _L0_ffn_in['signatures_raw'], 'L0_ffn_knot_values': _L0_ffn_in['knot_values'], 'L0_ffn_temperature': _L0_ffn_in['temperature'], 'L0_ffn_compress_w1': _L0_ffn_in['compress_w1'], 'L0_ffn_compress_b1': _L0_ffn_in['compress_b1'], 'L0_ffn_compress_w2': _L0_ffn_in['compress_w2'], 'L0_ffn_compress_b2': _L0_ffn_in['compress_b2'], 'L0_ffn_spline_w1': _L0_ffn_in['spline_w1'], 'L0_ffn_spline_b1': _L0_ffn_in['spline_b1'], 'L0_ffn_spline_w2': _L0_ffn_in['spline_w2'], 'L0_ffn_spline_b2': _L0_ffn_in['spline_b2'], 'L0_ffn_directions': _L0_ffn_in['directions'], 'L0_ffn_norm_gamma': _L0_ffn_in['norm_gamma'], 'L0_ffn_norm_beta': _L0_ffn_in['norm_beta'], 'L0_ffn_output_scale': _L0_ffn_in['output_scale']}

def reference(x, ctx_1024, mask_BxS2_bf0, L0_attn_scaling, L0_attn_qkv_w, L0_attn_qkv_b, L0_attn_o_w, L0_attn_o_b, L0_xattn_Wq, L0_xattn_bq, L0_xattn_Wkv, L0_xattn_bkv, L0_xattn_Wout, L0_xattn_bout, L0_ffn_signatures_raw, L0_ffn_knot_values, L0_ffn_temperature, L0_ffn_compress_w1, L0_ffn_compress_b1, L0_ffn_compress_w2, L0_ffn_compress_b2, L0_ffn_spline_w1, L0_ffn_spline_b1, L0_ffn_spline_w2, L0_ffn_spline_b2, L0_ffn_directions, L0_ffn_norm_gamma, L0_ffn_norm_beta, L0_ffn_output_scale):
    import jax
    import jax.numpy as jnp

    def _L0_attn_ref(hidden_states, scaling, qkv_w, qkv_b, o_w, o_b):
        import jax, jax.numpy as jnp
        import numpy as np
        NUM_HEADS = 16
        NUM_KV_HEADS = 4
        HEAD_DIM = 64
        HIDDEN = 256
        R_SOFTPLUS_0 = 1.442695041
        B, S, _ = hidden_states.shape
        H, KV, D = (NUM_HEADS, NUM_KV_HEADS, HEAD_DIM)
        rep = H // KV
        qkv = hidden_states @ qkv_w.T + qkv_b
        xq, xk, xv = jnp.split(qkv, [H * D, H * D + KV * D], axis=-1)
        xq = xq.reshape(B, S, H, D)
        xk = xk.reshape(B, S, KV, D)
        xv = xv.reshape(B, S, KV, D)
        scale = R_SOFTPLUS_0 / jnp.sqrt(jnp.float32(D)) * jax.nn.softplus(scaling)
        xq = xq * scale[None, None, None, :]
        xk = jnp.repeat(xk, rep, axis=2)
        xv = jnp.repeat(xv, rep, axis=2)
        scores = jnp.einsum('bqhd,bkhd->bhqk', xq, xk)
        probs = jax.nn.softmax(scores.astype(jnp.float32), axis=-1).astype(xq.dtype)
        out = jnp.einsum('bhqk,bkhd->bqhd', probs, xv)
        out = out.reshape(B, S, H * D)
        return out @ o_w.T + o_b

    def _L0_xattn_ref(query, context, mask, Wq, bq, Wkv, bkv, Wout, bout, num_heads):
        import jax, jax.numpy as jnp
        import numpy as np
        B, SQ, SKV, D, H = (2, 512, 512, 256, 16)
        HD = D // H

        def cross_attention(query, context, mask, Wq, bq, Wkv, bkv, Wout, bout, num_heads):
            b, sq, d = query.shape
            skv = context.shape[1]
            hd = d // num_heads
            scale = hd ** (-0.5)
            q = query @ Wq + bq
            kv = context @ Wkv + bkv
            kv = kv.reshape(b, skv, 2, num_heads, hd).transpose(2, 0, 3, 1, 4)
            k, v = (kv[0], kv[1])
            q = q.reshape(b, sq, num_heads, hd).transpose(0, 2, 1, 3)
            scores = jnp.einsum('bhid,bhjd->bhij', q, k) * scale
            scores = jnp.where(mask[:, None, None, :], -jnp.inf, scores)
            attn = jax.nn.softmax(scores, axis=-1)
            out = jnp.einsum('bhij,bhjd->bhid', attn, v)
            out = out.transpose(0, 2, 1, 3).reshape(b, sq, d)
            return out @ Wout + bout
        return cross_attention(query, context, mask, Wq, bq, Wkv, bkv, Wout, bout, num_heads)

    def _L0_ffn_ref(x, signatures_raw, knot_values, temperature, compress_w1, compress_b1, compress_w2, compress_b2, spline_w1, spline_b1, spline_w2, spline_b2, directions, norm_gamma, norm_beta, output_scale):
        import jax, jax.numpy as jnp
        import numpy as np
        D_MODEL = 256
        NUM_TILES = 64
        TPC = 8
        NUM_CLUSTERS = NUM_TILES // TPC
        GRID = 16
        COMP_H = 64
        NUM_KNOTS = 8
        EPS_LN = 1e-05

        def _calibrate(scores, knots, temperature):
            K = knots.shape[0]
            normalized = jax.nn.sigmoid(scores / (temperature[0] + 1e-06))
            idx_float = normalized * (K - 1)
            idx_low = jnp.clip(idx_float.astype(jnp.int32), 0, K - 2)
            idx_high = idx_low + 1
            t = idx_float - idx_low.astype(scores.dtype)
            val_low = knots[idx_low]
            val_high = knots[idx_high]
            return val_low + t * (val_high - val_low)

        def _forward(x, signatures_raw, knot_values, temperature, compress_w1, compress_b1, compress_w2, compress_b2, spline_w1, spline_b1, spline_w2, spline_b2, directions, norm_gamma, norm_beta, output_scale):
            B, T, D = x.shape
            xf = x.reshape(-1, D)
            q = jnp.where(signatures_raw > 0.3, 1.0, jnp.where(signatures_raw < -0.3, -1.0, 0.0)).astype(signatures_raw.dtype)
            sigs = signatures_raw + jax.lax.stop_gradient(q - signatures_raw)
            cluster_sigs = jnp.sign(sigs.reshape(NUM_CLUSTERS, TPC, D).mean(axis=1))
            cluster_scores = xf @ cluster_sigs.T
            cluster_gates = _calibrate(cluster_scores, knot_values, temperature)
            cluster_idx = jnp.argmax(cluster_gates, axis=-1)
            tile_scores = xf @ sigs.T
            tile_gates = _calibrate(tile_scores, knot_values, temperature)
            gates_by_cluster = tile_gates.reshape(-1, NUM_CLUSTERS, TPC)
            sel_gates = jnp.take_along_axis(gates_by_cluster, cluster_idx[:, None, None], axis=1)[:, 0, :]
            local_idx = jnp.argmax(sel_gates, axis=-1)
            tile_idx = cluster_idx * TPC + local_idx
            h = jax.nn.gelu(xf @ compress_w1 + compress_b1, approximate=False)
            comp = jnp.tanh(h @ compress_w2 + compress_b2)
            w1 = spline_w1[tile_idx]
            b1 = spline_b1[tile_idx]
            hh = jax.nn.relu(jnp.einsum('ni,nig->ng', comp, w1) + b1)
            w2 = spline_w2[tile_idx]
            b2 = spline_b2[tile_idx]
            mag = jnp.einsum('ng,ngo->no', hh, w2) + b2
            ffn_out = mag * directions[tile_idx] * output_scale[0]
            y = xf + ffn_out
            mu = y.mean(axis=-1, keepdims=True)
            var = ((y - mu) ** 2).mean(axis=-1, keepdims=True)
            y = (y - mu) / jnp.sqrt(var + EPS_LN) * norm_gamma + norm_beta
            return y.reshape(B, T, D)
        return _forward(x, signatures_raw, knot_values, temperature, compress_w1, compress_b1, compress_w2, compress_b2, spline_w1, spline_b1, spline_w2, spline_b2, directions, norm_gamma, norm_beta, output_scale)
    x = x + _L0_attn_ref(_layernorm(x, axis=-1), L0_attn_scaling, L0_attn_qkv_w, L0_attn_qkv_b, L0_attn_o_w, L0_attn_o_b)
    x = x + _L0_xattn_ref(_layernorm(x, axis=-1), ctx_1024, mask_BxS2_bf0, L0_xattn_Wq, L0_xattn_bq, L0_xattn_Wkv, L0_xattn_bkv, L0_xattn_Wout, L0_xattn_bout, 16)
    x = x + _L0_ffn_ref(_layernorm(x, axis=-1), L0_ffn_signatures_raw, L0_ffn_knot_values, L0_ffn_temperature, L0_ffn_compress_w1, L0_ffn_compress_b1, L0_ffn_compress_w2, L0_ffn_compress_b2, L0_ffn_spline_w1, L0_ffn_spline_b1, L0_ffn_spline_w2, L0_ffn_spline_b2, L0_ffn_directions, L0_ffn_norm_gamma, L0_ffn_norm_beta, L0_ffn_output_scale)
    return x

_drawn_inputs = setup_inputs


def setup_inputs(seed=0):
    import zlib

    import numpy as np

    out = dict(_drawn_inputs(seed))
    spreads = {'L0_xattn_bq': (0.0, 0.37),
     'L0_xattn_bkv': (0.0, 0.1),
     'L0_xattn_bout': (0.0, 0.1),
     'L0_ffn_compress_b1': (0.0, 0.8),
     'L0_ffn_compress_b2': (0.0, 2.0),
     'L0_ffn_spline_b1': (0.0, 2.0),
     'L0_ffn_spline_b2': (0.0, 2.0),
     'L0_ffn_norm_gamma': (1.0, 0.2),
     'L0_ffn_norm_beta': (0.0, 0.1)}
    factors = {'L0_attn_qkv_b': 5.901,
     'L0_attn_o_b': 6.04,
     'L0_ffn_signatures_raw': 8.0,
     'L0_ffn_knot_values': 8.0,
     'L0_ffn_compress_w1': 8.0,
     'L0_ffn_compress_w2': 8.0,
     'L0_ffn_spline_w1': 8.0,
     'L0_ffn_spline_w2': 8.0,
     'L0_ffn_directions': 8.0}
    for name, (base, spread) in spreads.items():
        noise = np.random.default_rng([zlib.crc32(name.encode()), seed]).standard_normal(out[name].shape)
        drawn = base * np.exp(spread * noise) if base else spread * noise
        out[name] = jnp.asarray(drawn.astype(out[name].dtype))
    for name, factor in factors.items():
        out[name] = (out[name] * factor).astype(out[name].dtype)
    return out
```

```python
from contextlib import ExitStack

import concourse.bass as bass
from concourse import mybir

F32 = mybir.dt.float32
F32R = mybir.dt.float32r
U8 = mybir.dt.uint8
ALU = mybir.AluOpType
ACT = mybir.ActivationFunctionType
AX = mybir.AxisListType

P = 128
B, S, D = 4, 1024, 256
H, HD, KV = 16, 64, 4
CH = 512
NT = CH // P
CHUNKS = B * S // CH
PER_BATCH = S // CH
KC = D // P
KT = S // P
PAIRS = H // 2
UNITS = CHUNKS * PAIRS
SC = 64
XH = 16
XHD = D // XH
HB = P // XHD
CL, TPC = 8, 8
TILES = CL * TPC
GRID, COMP, KNOTS = 16, 64, 8
SMALL = 4 * GRID + 2
EPS = 1e-5
R_SOFTPLUS_0 = 1.442695041

EARLY, LATE = "early", "late"
ALONE = "alone"

PE, ACTE, DVE, POOL, SP = "tensor", "scalar", "vector", "gpsimd", "sync"

COLUMNS = [("q_bias", PAIRS), ("k_bias", KV // 2), ("bq2", KC), ("bk2", KC), ("scaling", 1), ("cb1", 1)]
ROWS = [("v_bias", KV * HD), ("o_bias", D), ("bout2", D), ("gamma", D), ("beta", D), ("cb2", 2), ("knots", KNOTS),
        ("temperature", 1), ("out_scale", 1)]

ROWS_N = sum(n for _, n in ROWS)

INPUTS = [
    ("columns", (P, sum(n for _, n in COLUMNS))),
    ("rows", (1, sum(n for _, n in ROWS))),
    ("setup_rows", (1, D + HD)),
    ("x", (B * S, D)),
    ("ctxT", (D, B * SC)),
    ("mask", (1, B * SC // 4)),
    ("qkv_wT", (D, (H + 2 * KV) * HD)),
    ("o_wT", (H * HD, D)),
    ("Wq", (D, D)),
    ("Wkv", (D, 2 * D)),
    ("Wout", (D, D)),
    ("sigT", (D, TILES)),
    ("cw1", (D, COMP)),
    ("cw2", (COMP, 2)),
    ("sw1", (TILES, 2 * GRID)),
    ("sb1", (TILES, GRID)),
    ("sw2", (TILES, GRID)),
    ("sb2", (TILES, 1)),
    ("directions", (TILES, D)),
    ("consts", (P, P + 16 + HB)),
]


class Queues:

    def __init__(self, nc, ctx):
        self.nc, self.ctx = nc, ctx
        self.semaphores, self.count = {}, {}
        self.queue = {e: [] for e in (PE, ACTE, DVE, POOL, SP)}
        self.waited = {e: {} for e in self.queue}

    def put(self, engine, stage, instruction, *tokens, dma=False):
        waits = []
        for token in tokens:
            if token is None:
                continue
            name, value = token
            if self.waited[engine].get(name, 0) < value:
                self.waited[engine][name] = value
                waits.append((name, value))
        token = None
        if stage is not None:
            if stage not in self.count:
                self.semaphores[stage] = self.ctx.enter_context(self.nc.semaphore(stage))
                self.count[stage] = 0
            self.count[stage] += 16 if dma else 1
            token = (stage, self.count[stage])
        self.queue[engine].append((waits, instruction, stage, 16 if dma else 1))
        return token

    def play(self, engine, eng):
        for waits, instruction, stage, by in self.queue[engine]:
            for name, value in waits:
                eng.wait_ge(self.semaphores[name], value)
            done = instruction(eng)
            if stage is not None:
                done.then_inc(self.semaphores[stage], by)


class Ring:

    def __init__(self, buffers):
        self.buffers, self.at = buffers, -1
        self.readers = [[] for _ in buffers]

    def take(self):
        self.at = (self.at + 1) % len(self.buffers)
        readers, self.readers[self.at] = self.readers[self.at], None
        assert readers is not None, "a buffer is taken before its readers are known"
        return self.at, self.buffers[self.at], readers

    def free(self, at, *tokens):
        self.readers[at] = list(tokens)


def build(nc, ins, out):
    with ExitStack() as ctx:
        q = Queues(nc, ctx)
        put = q.put

        pool_done = [None]

        def pool(stage, instruction, *tokens):
            pool_done[0] = put(POOL, stage, instruction, *tokens, pool_done[0])
            return pool_done[0]

        def sb(name, shape, dtype=F32):
            return ctx.enter_context(nc.sbuf_tensor(name, shape, dtype))

        def bank(name, banks=1):
            return ctx.enter_context(nc.psum_tensor(name, [P, banks * 512], F32))

        max_scores = Ring([bank(f"max_scores{i}") for i in range(3)])
        key_scores = Ring([bank(f"key_scores{i}") for i in range(2)])
        attended = bank("attended")
        misc = Ring([bank(f"misc{i}") for i in range(2)])

        consts = sb("consts_sb", [P, P + 16 + HB])
        ident = consts[:, 0:P]
        knot_row = consts[:, P:P + 8]
        rank_row = consts[:, P + 8:P + 16]
        head_block = consts[:, P + 16:P + 16 + HB]
        ones = sb("ones", [P, HD])

        def views(name, parts):
            tile, at, found = sb(name, [P, sum(n for _, n in parts)]), 0, []
            for _, n in parts:
                found.append(tile[:, at:at + n])
                at += n
            return tile, found

        columns, (q_bias, k_bias, bq2, bk2, scaling_column, cb1) = views("columns_sb", COLUMNS)
        rows_sb, (v_bias, o_bias, bout2, gamma, beta, cb2, knots, temperature, out_scale) = views("rows_sb", ROWS)
        minus_half = sb("minus_half", [P, NT])

        wq_hl = sb("wq_hl", [P, 2, KC, H * HD], F32R)
        wk_hl = sb("wk_hl", [P, 2, KC, KV * HD], F32R)
        wv_hl = sb("wv_hl", [P, 2, KC, KV * HD], F32R)
        wo = sb("wo", [P, PAIRS, D])

        x_in = sb("x_in", [P, NT, D])
        xT = Ring([sb(f"xT{i}", [P, 2, KC, CH], F32R) for i in range(3)])
        k_high = sb("k_high", [P, KV, S], F32R)
        k_low = sb("k_low", [P, KV, S], F32R)
        v_all = sb("v_all", [P, KT, KV * HD])
        q_hl = [sb(f"q_hl{i}", [P, 2, CH], F32R) for i in range(3)]
        q_max = [sb(f"q_max{i}", [P, 2, CH], F32R) for i in range(2)]
        minus_max = [sb(f"minus_max{i}", [P, NT, 34]) for i in range(2)]
        probs = Ring([sb(f"probs{i}", [P, CH]) for i in range(6)])
        prob_sum = [sb(f"prob_sum{i}", [P, CH]) for i in range(2)]
        inv_sum = sb("inv_sum", [P, CH])
        raw_out = sb("raw_out", [P, CH])
        heads_out = sb("heads_out", [P, PAIRS, CH])

        wq2 = sb("wq2", [P, KC, D])
        wout2 = sb("wout2", [P, KC, D])
        k2T = sb("k2T", [P, KC, B * SC])
        k2_block = sb("k2_block", [P, KC, HB, SC])
        v2_block = sb("v2_block", [P, B, XH // 2, 2, XHD])
        mask_add = sb("mask_add", [P, B * SC])

        route_w = sb("route_w", [P, KC, CL + TILES])
        cw1 = sb("cw1_sb", [P, KC, COMP])
        cw2 = sb("cw2_sb", [COMP, 2])
        table = sb("table", [TILES, SMALL + D])
        knot_step = sb("knot_step", [P, KNOTS - 1])
        inv_temp = sb("inv_temp", [P, 1])

        stats = sb("stats", [P, NT, 6])
        moments = sb("moments", [P, NT, 2])
        rstd = sb("rstd", [P, 2, NT])
        buf_a = sb("buf_a", [P, NT, D])
        buf_b = sb("buf_b", [P, NT, D])
        buf_c = sb("buf_c", [P, KC, CH])
        buf_d = sb("buf_d", [P, KC * CH])
        weights = Ring([sb(f"weights{i}", [P, CH]) for i in range(2)])
        row_stat = sb("row_stat", [P, 3, HB])
        p2T = sb("p2T", [P, 4, CH // 2])
        hT = p2T[0:COMP, 0:2, :].rearrange("p a b -> p (a b)")
        pickT = p2T[0:TILES, 2:4, :].rearrange("p a b -> p (a b)")
        route = sb("route", [P, NT, CL + TILES])
        comp = sb("comp", [P, 3, NT, 2])
        small = sb("small", [P, NT, SMALL])
        words = NT * CL * 8
        part = lambda n, size: buf_c[:, :, :].rearrange("p a b -> p (a b)")[:, n * words:n * words + size]
        gate = part(0, words).rearrange("p (k i c) -> p k i c", k=8, i=NT)
        intervals = part(1, words).rearrange("p (n k) -> p n k", k=KNOTS)
        picked_by = part(2, words).rearrange("p (i c t) -> p i c t", i=NT, c=CL)
        hidden = part(3, 2 * NT * GRID).rearrange("p (a i n) -> p a i n", a=2, i=NT)
        mag = sb("mag", [P, NT])

        def exp_set():
            put(ACTE, None, lambda e: e.preload_act_table_set("natural_log_exp_and_others"))

        exp_set()
        loads = {}

        def load(name, dst, src, *tokens):
            loads[name] = put(SP, f"load_{name}", lambda e: e.dma_start(dst, src), *tokens, dma=True)
            return loads[name]

        load("consts", consts[:, :], ins["consts"])

        def load_x(t, dst, *tokens):
            rows = ins["x"][t * CH:(t + 1) * CH, :].rearrange("(i p) d -> p i d", p=P)
            return load("x_first" if dst is buf_a else "x_in", dst[:, :, :], rows, *tokens)

        x_loaded = {0: (x_in, load_x(0, x_in)), 1: (buf_a, load_x(1, buf_a))}
        staged = heads_out[:, :, :].rearrange("p a b -> p (a b)")[:, 0:KC * (H + 2 * KV) * HD]
        staged = staged.rearrange("p (c n) -> p c n", c=KC)
        load("qkv_w", staged, ins["qkv_wT"].rearrange("(c p) n -> p c n", p=P))
        load("columns", columns[:, :], ins["columns"])
        load("setup_rows", buf_b[:, 2:4, :].rearrange("p a b -> p (a b)")[:, 0:D + HD], ins["setup_rows"].broadcast_to([P, D + HD]))
        bv2 = buf_b[:, 2, :]
        load("rows", rows_sb[:, :], ins["rows"].broadcast_to([P, ROWS_N]))

        ones_set = put(DVE, "setup_v", lambda e: e.memset(ones[:, :], 1.0))
        def fill(view, value):
            return pool("fills", lambda e: e.memset(view, value))

        half_set = fill(minus_half[:, :], -0.5)

        def fill_padding():
            for i in range(2):
                fill(minus_max[i][:, :, :], 0.0)
                fill(q_max[i][HD:P, :, :].bitcast(F32), 0.0)
            fill(k_low[HD:P, :, :].bitcast(F32), 0.0)
            fill(k_low[HD:HD + 1, :, :].bitcast(F32), 1.0)
            return fill(v2_block[:, :, :, :, :], 0.0)

        split = {}

        def split_weights(name, dst, at, *ready):
            src = staged[:, :, at:at + dst.shape[3]]
            high = put(DVE, "weights_high", lambda e: e.tensor_copy(dst[:, 0], src), loads["qkv_w"], *ready)
            split[name] = put(DVE, "weights_low", lambda e: e.tensor_tensor(
                dst[:, 1], src, dst[:, 0].bitcast(F32), ALU.subtract), high)

        def scale_q():
            def soft(k):
                return buf_c[:, :, :].rearrange("p a b -> p (a b)")[:, k * (HD + 1):(k + 1) * (HD + 1)]

            def vector(instruction, *tokens):
                return put(DVE, "softplus", instruction, *tokens)

            scaling, minus, least, e_, u_, log_u, u1 = [soft(k) for k in range(7)]
            g = vector(lambda e: e.tensor_copy(scaling[:, 0:HD], buf_b[:, 3, 0:HD]), loads["setup_rows"])
            g2 = vector(lambda e: e.tensor_copy(scaling[:, HD:HD + 1], scaling_column), loads["columns"])
            g = vector(lambda e: e.tensor_scalar(minus, scaling, -1.0, None, ALU.mult), g, g2)
            g = vector(lambda e: e.tensor_tensor(least, minus, scaling, ALU.min), g)
            g = put(ACTE, "softplus_exp", lambda e: e.activation(e_, least, ACT.Exp), g)
            g = vector(lambda e: e.tensor_scalar(u_, e_, 1.0, None, ALU.add), g)
            logged = put(ACTE, "softplus_ln", lambda e: e.activation(log_u, u_, ACT.Ln), g)
            rounded = vector(lambda e: e.tensor_scalar(u1, u_, -1.0, None, ALU.add), g)
            g = vector(lambda e: e.tensor_scalar(minus, u1, 1e-30, None, ALU.max), rounded)
            g = vector(lambda e: e.reciprocal(least, minus), g)
            g = vector(lambda e: e.tensor_tensor(minus, least, e_, ALU.mult), g)
            g = vector(lambda e: e.tensor_tensor(minus, minus, log_u, ALU.mult), g, logged)
            g = vector(lambda e: e.tensor_scalar(least, u1, 0.0, None, ALU.is_equal), g)
            g = vector(lambda e: e.tensor_tensor(least, least, e_, ALU.mult), g)
            g = vector(lambda e: e.tensor_tensor(minus, minus, least, ALU.add), g)
            g = vector(lambda e: e.scalar_tensor_tensor(
                out=least, in0=scaling, scalar=0.0, in1=minus, op0=ALU.max, op1=ALU.add), g)
            q_scale = minus
            scaled = vector(lambda e: e.tensor_scalar(q_scale, least, R_SOFTPLUS_0 / HD ** 0.5, None, ALU.mult), g)
            q_scaled = vector(lambda e: e.tensor_scalar(
                q_bias[:, :], q_bias[:, :], q_scale[:, HD:HD + 1], None, ALU.mult), scaled, loads["columns"])

            for c in range(KC):
                wq_scaled = staged[:, c, 0:H * HD].rearrange("p (h d) -> p h d", d=HD)
                q_weights = vector(lambda e, w=wq_scaled: e.tensor_tensor(
                    w, w, q_scale[:, 0:HD].unsqueeze(1).broadcast_to([P, H, HD]), ALU.mult), scaled, loads["qkv_w"])
            return q_scaled, q_weights

        norm_done = [None]

        def measure(src, *ready):
            tokens = []
            for i in range(NT):
                tokens.append(put(DVE, "bn_stats", lambda e, i=i: e.bn_stats(stats[:, i, :], src[:, i, :]),
                                  *ready, norm_done[0]))
            for i in range(NT):
                last = put(DVE, "bn_aggr", lambda e, i=i: e.bn_aggr(moments[:, i, :], stats[:, i, :]),
                           tokens[i], norm_done[0])
            add = pool("var_eps", lambda e: e.tensor_scalar(
                rstd[:, 0, :], moments[:, :, 1], EPS, None, ALU.add), last)
            root = pool("rstd", lambda e: e.tensor_tensor(
                rstd[:, 1, :], rstd[:, 0, :], minus_half[:, :], ALU.pow), add, half_set)
            return last, root

        def layer_norm(src, dst, *ready):
            _, root = measure(src, *ready)
            yield LATE
            for i in range(NT):
                norm_done[0] = put(DVE, "normed", lambda e, i=i: e.tensor_scalar(
                    dst[:, i, :], src[:, i, :], moments[:, i, 0:1], rstd[:, 1, i:i + 1],
                    ALU.subtract, ALU.mult), root)

        def half_op(half, stage, dst, a, b, op, *ready):
            tiles = slice(half * NT // 2, (half + 1) * NT // 2)
            other = b[:, tiles, :] if len(b.shape) == 3 else b.unsqueeze(1).broadcast_to([P, NT // 2, D])
            return pool(stage, lambda e: e.tensor_tensor(dst[:, tiles, :], a[:, tiles, :], other, op), *ready)

        def transposes(src, c, *ready):
            at, ps, free = misc.take()
            for i in range(NT):
                done = put(PE, "x_transposed" if i == NT - 1 else None, lambda e, i=i: e.transpose(
                    ps[:, i * P:(i + 1) * P], src[:, i, c * P:(c + 1) * P], ident), *ready, *free, loads["consts"])
            return at, ps, done

        x_ready, x_slot = {}, {}
        x_read = {}
        xT_readers = {}

        def prep(t):
            x_in, loaded = x_loaded[t]
            yield LATE
            yield from layer_norm(x_in, x_in, loaded)
            yield LATE
            yield EARLY
            slot, buf, free = xT.take()
            x_slot[t] = (slot, buf)
            xT_readers[t] = []
            for c in range(KC):
                at, ps, done = transposes(x_in, c, norm_done[0])
                yield LATE
                high = put(ACTE, "xT_high", lambda e, ps=ps, c=c: e.activation(buf[:, 0, c, :], ps[:, :], ACT.Copy), done, *free)
                low = put(DVE, "xT_low", lambda e, ps=ps, c=c: e.tensor_tensor(
                    buf[:, 1, c, :], ps[:, :], buf[:, 0, c, :].bitcast(F32), ALU.subtract), done, high, *free)
                misc.free(at, low)
                if c < KC - 1:
                    yield EARLY
            x_ready[t] = low
            x_read[t] = done
            follower = t + 1 if t else 2
            if t != 1 and follower < CHUNKS:
                x_loaded[follower] = x_in, load_x(follower, x_in, done)

        def three_products(ps_out, lhs, rhs, stage, *ready):
            terms = [(a, b, c) for c in range(KC) for a, b in ((0, 0), (0, 1), (1, 0))]
            for n, (a, b, c) in enumerate(terms):
                token = put(PE, stage if n == len(terms) - 1 else None, lambda e, a=a, b=b, c=c, n=n: e.matmul(
                    ps_out, lhs(a, c), rhs(b, c), start=n == 0, stop=n == len(terms) - 1), *ready)
            return token

        k_ready, v_ready = {}, {}
        k_read, v_read = {}, {}

        def project_k(b, half, c):
            t = b * PER_BATCH + c
            _, buf = x_slot[t]
            at, ps, free = misc.take()
            done = three_products(ps[:, :], lambda a, kc: wk_hl[:, a, kc, half * P:(half + 1) * P],
                                  lambda a, kc: buf[:, a, kc, :], "k_projected", *free, x_ready[t], split["k"])
            xT_readers[t].append(done)
            yield LATE
            cols = slice(c * CH, (c + 1) * CH)
            for head in range(2):
                g = 2 * half + head
                rows = slice(head * HD, (head + 1) * HD)
                for copy in range(2):
                    high = put(ACTE, "k_high", lambda e, g=g, r=rows, o=copy * HD: e.activation(
                        k_high[o:o + HD, g, cols], ps[r, :], ACT.Identity, bias=k_bias[r, half:half + 1]),
                        done, k_read.get(g), loads["columns"])
                low = put(DVE, "k_low", lambda e, g=g, r=rows: e.scalar_tensor_tensor(
                    out=k_low[0:HD, g, cols], in0=ps[r, :], scalar=k_bias[r, half:half + 1],
                    in1=k_high[r, g, cols].bitcast(F32), op0=ALU.add, op1=ALU.subtract), high)
                k_ready[b, g, c] = low
            misc.free(at, low)

        def project_v(b, half, c):
            t = b * PER_BATCH + c
            _, buf = x_slot[t]
            at, ps, free = misc.take()
            n = KV // 2 * HD
            for i in range(NT):
                done = three_products(
                    ps[:, i * n:(i + 1) * n], lambda a, kc, i=i: buf[:, a, kc, i * P:(i + 1) * P],
                    lambda a, kc: wv_hl[:, a, kc, half * n:(half + 1) * n], "v_projected", *free,
                    x_ready[t], split["v"])
            xT_readers[t].append(done)
            yield LATE
            token = put(DVE, "v_all", lambda e: e.tensor_tensor(
                v_all[:, c * NT:(c + 1) * NT, half * n:(half + 1) * n],
                ps[:, :].rearrange("p (i n) -> p i n", i=NT),
                v_bias[:, half * n:(half + 1) * n].unsqueeze(1).broadcast_to([P, NT, n]), ALU.add),
                done, loads["rows"], v_read.get(half))
            misc.free(at, token)
            v_ready[b, half, c] = token

        q_hl_ready, q_max_ready = {}, {}
        pass2_done, max_taken, shift_done = {}, {}, {}
        exps = {}
        sum_done = {}
        attended_free = [None]
        heads_ready = {}
        heads_read = {}

        def project_q(u):
            t, p = divmod(u, PAIRS)
            slot, buf = x_slot[t]
            dst = q_hl[u % 3]
            at, ps, free = misc.take()
            done = three_products(ps[:, :], lambda a, kc: wq_hl[:, a, kc, p * P:(p + 1) * P],
                                  lambda a, kc: buf[:, a, kc, :], "q_projected", *free, x_ready[t], split["q"])
            xT_readers[t].append(done)
            if p == PAIRS - 1:
                xT.free(slot, *xT_readers[t])
            yield LATE
            old = pass2_done.get(u - 3)
            for head in range(2):
                rows, other = slice(head * HD, (head + 1) * HD), slice((1 - head) * HD, (2 - head) * HD)
                high = put(ACTE, "q_high", lambda e, r=rows, h=head: e.activation(
                    dst[r, h, :], ps[r, :], ACT.Identity, bias=q_bias[r, p:p + 1]), done, q_scaled, old)
                low = put(DVE, "q_low", lambda e, r=rows, o=other, h=head: e.scalar_tensor_tensor(
                    out=dst[o, h, :], in0=ps[r, :], scalar=q_bias[r, p:p + 1], in1=dst[r, h, :].bitcast(F32),
                    op0=ALU.add, op1=ALU.subtract), high)
            misc.free(at, low)
            q_hl_ready[u] = low

        def take_max(u, i):
            t, p = divmod(u, PAIRS)
            b, g = t // PER_BATCH, p // 2
            head, tile = divmod(i, NT)
            src, dst = q_hl[u % 3], minus_max[u % 2]
            for half in range(2):
                at, ps, free = max_scores.take()
                done = put(PE, "max_scores", lambda e, half=half, ps=ps: e.matmul(
                    ps[:, :], src[:, head, tile * P:(tile + 1) * P],
                    k_high[:, g, half * 512:(half + 1) * 512], start=True, stop=True),
                    q_hl_ready[u], k_ready[b, g, 0], k_ready[b, g, 1], *free)
                column = 32 * head + half
                token = put(DVE, "minus_max", lambda e, c=column, ps=ps: e.tensor_reduce(
                    dst[:, tile, c:c + 1], ps[:, :], AX.X, ALU.max, negate=True),
                    done, shift_done.get(u - 2), filled)
                max_scores.free(at, token)
            if i == 2 * NT - 1:
                max_taken[u] = put(DVE, "both_halves", lambda e: e.tensor_tensor(
                    dst[:, :, 0::32], dst[:, :, 0::32], dst[:, :, 1::32], ALU.min), token)

        def shift_rows(u):
            src, high, dst = minus_max[u % 2], q_hl[u % 3], q_max[u % 2]
            old = pass2_done.get(u - 2)
            for head in range(2):
                yield LATE
                rows = slice(head * HD, (head + 1) * HD)
                again = pool("q_high_again", lambda e, h=head, r=rows: e.tensor_copy(
                    dst[0:HD, h, :], high[r, h, :].bitcast(F32)), q_hl_ready[u], old)
            yield EARLY
            at, ps, free = misc.take()
            for i in range(NT):
                done = put(PE, "max_transposed" if i == NT - 1 else None, lambda e, i=i: e.transpose(
                    ps[0:34, i * P:(i + 1) * P], src[:, i, :], ident), max_taken[u], *free, loads["consts"])
            shift_done[u] = done
            yield LATE
            tokens = [again]
            for head in range(2):
                tokens.append(put(ACTE, "max_row", lambda e, h=head: e.activation(
                    dst[HD:HD + 1, h, :], ps[32 * h:32 * h + 1, :], ACT.Copy), done, old, filled))
            misc.free(at, tokens[-1])
            q_max_ready[u] = tokens

        def score_keys(u, kt):
            t, p = divmod(u, PAIRS)
            b, g = t // PER_BATCH, p // 2
            high, shifted = q_hl[u % 3], q_max[u % 2]
            keys = slice(kt * P, (kt + 1) * P)
            for head in range(2):
                at, ps, free = key_scores.take()
                put(PE, None, lambda e, h=head, ps=ps: e.matmul(
                    ps[:, :], k_high[:, g, keys], high[:, h, :], start=True, stop=False), *free,
                    q_hl_ready[u], k_ready[b, g, 0], k_ready[b, g, 1])
                done = put(PE, "key_scores", lambda e, h=head, ps=ps: e.matmul(
                    ps[:, :], k_low[:, g, keys], shifted[:, h, :], start=False, stop=True),
                    *q_max_ready[u], filled)
                slot, buf, readers = probs.take()
                token = put(ACTE, "exp", lambda e, ps=ps, buf=buf: e.activation(buf[:, :], ps[:, :], ACT.Exp),
                            done, *readers)
                key_scores.free(at, token)
                exps[u, kt, head] = (slot, buf, token)
            pass2_done[u] = done
            k_read[g] = done

        def attend(u, kt):
            t, p = divmod(u, PAIRS)
            b, half = t // PER_BATCH, p // 4
            g = p // 2
            pv = []
            for head in range(2):
                slot, buf, token = exps[u, kt, head]
                pv.append(put(PE, "attended", lambda e, h=head, buf=buf: e.matmul(
                    attended[h * HD:(h + 1) * HD, :], v_all[:, kt, g * HD:(g + 1) * HD], buf[:, :],
                    start=kt == 0, stop=kt == KT - 1), token, v_ready[b, half, 0], v_ready[b, half, 1],
                    attended_free[0] if kt == 0 else None))
            v_read[half] = pv[1]
            if kt == KT - 1:
                attended_free[0] = put(ACTE, "raw_out", lambda e: e.activation(
                    raw_out[:, :], attended[:, :], ACT.Copy), pv[1], heads_ready.get(u - 1))
            if kt == 0:
                return
            for head in range(2):
                add = (lambda *a: put(DVE, *a), pool)[head]
                slot, buf, token = exps[u, kt, head]
                acc = prob_sum[head]
                if kt == 1:
                    first_slot, first, first_token = exps[u, 0, head]
                    done = add(f"prob_sum{head}", lambda e, a=acc, x=first, y=buf: e.tensor_tensor(
                        a[:, :], x[:, :], y[:, :], ALU.add), first_token, token, sum_done.get(u - 1))
                    probs.free(first_slot, done, pv[head])
                else:
                    done = add(f"prob_sum{head}", lambda e, a=acc, y=buf: e.tensor_tensor(
                        a[:, :], a[:, :], y[:, :], ALU.add), token, sum_token[head])
                sum_token[head] = done
                probs.free(slot, done, pv[head])

        sum_token = [None, None]

        def finish(u):
            t, p = divmod(u, PAIRS)
            at, ps, free = misc.take()
            for head in range(2):
                done = put(PE, "sums", lambda e, h=head: e.matmul(
                    ps[h * HD:(h + 1) * HD, :], ones[:, :], prob_sum[h][:, :], start=True, stop=True),
                    sum_token[head], *free, ones_set)
            sum_done[u] = done
            yield LATE
            ln = put(ACTE, "ln_sum", lambda e: e.activation(inv_sum[:, :], ps[:, :], ACT.Ln), done, heads_ready.get(u - 1))
            misc.free(at, ln)
            inv = put(ACTE, "inv_sum", lambda e: e.activation(inv_sum[:, :], inv_sum[:, :], ACT.Exp, scale=-1.0), ln)
            yield LATE
            token = pool("heads_out", lambda e: e.tensor_tensor(
                heads_out[:, p, :], raw_out[:, :], inv_sum[:, :], ALU.mult), attended_free[0], inv, heads_read.get(p), split["v"])
            heads_ready[u] = token

        tail_free = {"a": None, "c": [], "d": None, "p2T": None}
        stored = {}

        def tail(t):
            b = t // PER_BATCH
            rows = slice(t * CH, (t + 1) * CH)
            x_rows = ins["x"][rows, :].rearrange("(i p) d -> p i d", p=P)
            xl = load("residual", buf_a[:, :, :], x_rows, stored.get(t - 1), tail_free["a"])
            yield EARLY
            for i in range(NT):
                at, ps, free = misc.take()
                for p in range(PAIRS):
                    done = put(PE, "projected" if p == PAIRS - 1 else None, lambda e, p=p, i=i, ps=ps: e.matmul(
                        ps[:, 0:D], heads_out[:, p, i * P:(i + 1) * P], wo[:, p, :], start=p == 0, stop=p == PAIRS - 1),
                        *free, heads_ready[t * PAIRS + p], loads["wo"])
                if i == NT - 1:
                    for p in range(PAIRS):
                        heads_read[p] = done
                yield LATE
                if i < 2:
                    biased = half_op(i, "residual_bias", buf_a, buf_a, o_bias[:, :], ALU.add, xl, loads["rows"])
                x1 = put(DVE, "x1", lambda e, i=i, ps=ps: e.tensor_tensor(
                    buf_a[:, i, :], ps[:, 0:D], buf_a[:, i, :], ALU.add), done, biased)
                misc.free(at, x1)
                yield EARLY if i < NT - 1 else LATE
            yield from layer_norm(buf_a, buf_b, x1, stored.get(t - 1))
            normed = norm_done[0]
            yield EARLY
            for c in range(KC):
                at, ps, done = transposes(buf_b, c, normed)
                yield LATE
                a_bias = half_op(c, "output_bias", buf_a, buf_a, bout2[:, :], ALU.add, normed, loads["rows"])
                ct = put(ACTE, "normT", lambda e, c=c, ps=ps: e.activation(buf_c[:, c, :], ps[:, :], ACT.Copy),
                         done, *tail_free["c"])
                misc.free(at, ct)
                yield EARLY
            if t % PER_BATCH == 0:
                for m in range(KC):
                    k2_done = pool("k2_block", lambda e, m=m: e.tensor_tensor(
                        k2_block[:, m, :, :], k2T[:, m, b * SC:(b + 1) * SC].unsqueeze(1).broadcast_to([P, HB, SC]),
                        head_block.unsqueeze(2).broadcast_to([P, HB, SC]), ALU.mult),
                        k2_ready, tail_free.get("k2"))
                tail_free["k2_ready"] = k2_done
            k2_done = tail_free["k2_ready"]
            for m in range(KC):
                at, ps, free = misc.take()
                for c in range(KC):
                    done = put(PE, "q2" if c else None, lambda e, m=m, c=c, ps=ps: e.matmul(
                        ps[:, :], wq2[:, c, m * P:(m + 1) * P], buf_c[:, c, :], start=c == 0, stop=c == 1),
                        *free, ct, loads["wq2"])
                yield LATE
                qd = put(ACTE, "q2_done", lambda e, m=m, ps=ps: e.activation(
                    buf_d[:, m * CH:(m + 1) * CH], ps[:, :], ACT.Identity, scale=XHD ** -0.5, bias=bq2[:, m:m + 1]),
                    done, bq2_ready, tail_free["d"])
                misc.free(at, qd)
                yield EARLY
            tail_free["c"] = [done]
            tiles = [(m, i) for m in range(KC) for i in range(NT)]
            p2_free = tail_free["p2T"]
            soft, normal = {}, {}
            for n in range(len(tiles) + 2):
                if n < len(tiles):
                    m, i = tiles[n]
                    at, ps, free = misc.take()
                    scored = put(PE, "scores2", lambda e, m=m, i=i, ps=ps: e.matmul(
                        ps[:, :], buf_d[:, m * CH + i * P:m * CH + (i + 1) * P],
                        k2_block[:, m, :, :].rearrange("p a b -> p (a b)"), start=True, stop=True),
                        *free, qd, k2_done)
                pair_done = n >= 3 and n % 2 == 1
                if pair_done:
                    m, i = tiles[n - 3]
                    at2, ps2, free = misc.take()
                    for j in range(4):
                        done = put(PE, "attended2", lambda e, j=j, m=m, ps=ps2: e.matmul(
                            ps[32 * j:32 * j + 32, 0:CH // 2],
                            v2_block[:, b, 4 * m + j, :, :].rearrange("p a b -> p (a b)"), p2T[:, j, :],
                            start=True, stop=True), *free, ev, v2_ready)
                    p2_free = done
                if n != len(tiles):
                    yield LATE
                if pair_done:
                    ot = put(ACTE, "out2T", lambda e, m=m, i=i, ps=ps2: e.activation(
                        buf_d[:, m * CH + i * P:m * CH + (i + 2) * P], ps[:, 0:CH // 2], ACT.Copy), done)
                    misc.free(at2, ot)
                if n < len(tiles):
                    slot, w, w_free = weights.take()
                    w3 = w[:, :].rearrange("p (h k) -> p h k", h=HB)
                    s = put(DVE, "soft2", lambda e, ps=ps, w3=w3: e.tensor_tensor(
                        w3, ps[:, :].rearrange("p (h k) -> p h k", h=HB),
                        mask_add[:, b * SC:(b + 1) * SC].unsqueeze(1).broadcast_to([P, HB, SC]), ALU.add),
                        scored, mask_ready, *w_free)
                    misc.free(at, s)
                    mx = put(DVE, "soft2", lambda e, w3=w3: e.tensor_reduce(
                        row_stat[:, 0, :], w3, AX.X, ALU.max), s, q_scaled)
                    less = put(DVE, "soft2", lambda e, w3=w3: e.tensor_tensor(
                        w3, w3, row_stat[:, 0, :].unsqueeze(2).broadcast_to([P, HB, SC]), ALU.subtract), mx)
                    soft[n] = (slot, w, w3)
                if n > len(tiles):
                    break
                if n < len(tiles):
                    yield EARLY
                    ex = put(ACTE, "exp2", lambda e, w=w: e.activation(w[:, :], w[:, :], ACT.Exp), less)
                transposing = 1 <= n <= len(tiles)
                if transposing:
                    _, i = tiles[n - 1]
                    before, w, _ = soft[n - 1]
                    at, ps, free = misc.take()
                    for j in range(4):
                        done = put(PE, "weights2T" if j == 3 else None, lambda e, j=j, w=w, ps=ps: e.transpose(
                            ps[:, j * P:(j + 1) * P], w[:, j * P:(j + 1) * P], ident), *free, normal[n - 1])
                    weights.free(before, done)
                yield LATE
                if transposing:
                    ev = put(ACTE, "p2T", lambda e, i=i, ps=ps: e.activation(
                        p2T[:, :, (i % 2) * P:(i % 2 + 1) * P], ps[:, :].rearrange("p (j n) -> p j n", j=4), ACT.Copy),
                        done, p2_free)
                    misc.free(at, ev)
                if n < len(tiles):
                    _, _, w3 = soft[n]
                    sm = put(DVE, "soft2", lambda e, w3=w3: e.tensor_reduce(
                        row_stat[:, 1, :], w3, AX.X, ALU.add), ex)
                    sm = put(DVE, "soft2", lambda e: e.reciprocal(row_stat[:, 2, :], row_stat[:, 1, :]), sm, tail_free.get("rs"))
                    normal[n] = tail_free["rs"] = pool("weights2", lambda e, w3=w3: e.tensor_tensor(
                        w3, w3, row_stat[:, 2, :].unsqueeze(2).broadcast_to([P, HB, SC]), ALU.mult), sm)
                yield ALONE if n >= 2 and n % 2 == 0 and n < len(tiles) else EARLY
            yield EARLY
            tail_free["k2"] = done
            tail_free["p2T"] = done
            for pair in range(NT // 2):
                at, ps, free = misc.take()
                for i in range(2):
                    for m in range(KC):
                        col = m * CH + (2 * pair + i) * P
                        done = put(PE, "projected2" if m else None, lambda e, m=m, i=i, col=col, ps=ps: e.matmul(
                            ps[:, i * D:(i + 1) * D], buf_d[:, col:col + P], wout2[:, m, :],
                            start=m == 0, stop=m == 1), *free, ot, loads["wout2"])
                yield LATE
                tile_pair = buf_a[:, 2 * pair:2 * pair + 2, :]
                x2 = put(DVE, "x2", lambda e, dst=tile_pair, ps=ps: e.tensor_tensor(
                    dst, ps[:, :].rearrange("p (i d) -> p i d", i=2), dst, ALU.add), done, a_bias)
                misc.free(at, x2)
                yield EARLY if pair == 0 else LATE
            d_free = done
            yield from layer_norm(buf_a, buf_b, x2)
            normed = norm_done[0]
            yield LATE
            yield EARLY
            for c in range(KC):
                at, ps, done = transposes(buf_b, c, normed)
                yield LATE
                ct = put(ACTE, "normT", lambda e, c=c, ps=ps: e.activation(buf_c[:, c, :], ps[:, :], ACT.Copy),
                         done, *tail_free["c"])
                misc.free(at, ct)
                yield EARLY
            at, ps, free = misc.take()
            n = CL + TILES
            for i in range(NT):
                for c in range(KC):
                    done = put(PE, "route_scores" if c else None, lambda e, i=i, c=c, ps=ps: e.matmul(
                        ps[:, i * n:(i + 1) * n], buf_c[:, c, i * P:(i + 1) * P], route_w[:, c, :],
                        start=c == 0, stop=c == 1), *free, ct, route_w_ready)
            yield LATE
            rs = put(ACTE, "route", lambda e, ps=ps: e.activation(
                route[:, :, :], ps[:, 0:NT * n].rearrange("p (i n) -> p i n", i=NT), ACT.Copy), done, tail_free.get("route"))
            misc.free(at, rs)
            yield EARLY
            at, ps, free = misc.take()
            for c in range(KC):
                done = put(PE, "compressed" if c else None, lambda e, c=c, ps=ps: e.matmul(
                    ps[0:COMP, :], cw1[:, c, :], buf_c[:, c, :], start=c == 0, stop=c == 1), *free, loads["cw1"])
            c_read = done
            yield LATE
            ge = put(ACTE, "gelu", lambda e, ps=ps: e.activation(
                hT, ps[0:COMP, :], ACT.Gelu, bias=cb1[0:COMP, 0:1]), done, loads["columns"], tail_free["p2T"])
            exp_set()
            misc.free(at, ge)
            yield EARLY
            at, ps, free = misc.take()
            for i in range(NT):
                done = put(PE, "comp" if i == NT - 1 else None, lambda e, i=i, ps=ps: e.matmul(
                    ps[:, 2 * i:2 * i + 2], hT[:, i * P:(i + 1) * P], cw2[:, :], start=True, stop=True),
                    *free, ge, loads["cw2"])
            yield LATE
            cal = [None]

            def calibrate(src, dst, *ready):
                flat = lambda k: gate[:, k].rearrange("p a b -> p (a b)")
                g = put(DVE, "gate", lambda e: e.tensor_scalar(
                    gate[:, 0], src, inv_temp[:, 0:1], 88.0, ALU.mult, ALU.min), *ready, temp_ready)
                yield EARLY
                g = put(ACTE, "gate_exp", lambda e: e.activation(gate[:, 0], gate[:, 0], ACT.Exp), g)
                yield LATE
                g = put(DVE, "gate", lambda e: e.tensor_scalar(gate[:, 0], gate[:, 0], 1.0, None, ALU.add), g)
                g = put(DVE, "gate", lambda e: e.reciprocal(gate[:, 1], gate[:, 0]), g)
                f = put(DVE, "gate", lambda e: e.tensor_scalar(gate[:, 0], gate[:, 1], KNOTS - 1.0, None, ALU.mult), g)
                g = put(DVE, "gate", lambda e: e.tensor_tensor(
                    intervals[:, :, :], flat(0).unsqueeze(2).broadcast_to([P, NT * CL, KNOTS]),
                    knot_row.unsqueeze(1).broadcast_to([P, NT * CL, KNOTS]), ALU.is_ge), f)
                low = put(DVE, "gate", lambda e: e.tensor_reduce(
                    flat(1), intervals[:, :, 1:KNOTS], AX.X, ALU.add), g)
                t_ = put(DVE, "gate", lambda e: e.tensor_tensor(gate[:, 0], gate[:, 0], gate[:, 1], ALU.subtract), low)
                yield LATE
                one = put(DVE, "gate", lambda e: e.tensor_tensor(
                    intervals[:, :, 0:KNOTS - 1], intervals[:, :, 0:KNOTS - 1], intervals[:, :, 1:KNOTS],
                    ALU.subtract), t_)
                for k, values in ((1, knots[:, 0:KNOTS - 1]), (2, knot_step[:, :])):
                    pick = put(DVE, "gate", lambda e, values=values: e.tensor_tensor(
                        picked(values), intervals[:, :, 0:KNOTS - 1],
                        values.unsqueeze(1).broadcast_to([P, NT * CL, KNOTS - 1]), ALU.mult), one, temp_ready)
                    one = put(DVE, "gate", lambda e, k=k: e.tensor_reduce(flat(k), picked(None), AX.X, ALU.add), pick)
                g = put(DVE, "gate", lambda e: e.tensor_tensor(gate[:, 0], gate[:, 0], gate[:, 2], ALU.mult), one)
                cal[0] = put(DVE, "gate", lambda e: e.tensor_tensor(dst, gate[:, 0], gate[:, 1], ALU.add), g)

            def picked(_):
                return picked_by[:, :, :, :].rearrange("p a b c -> p (a b) c")[:, :, 0:KNOTS - 1]

            z = put(DVE, "tanh", lambda e, ps=ps: e.tensor_tensor(
                comp[:, 0], ps[:, 0:2 * NT].rearrange("p (i n) -> p i n", i=NT),
                cb2[:, :].unsqueeze(1).broadcast_to([P, NT, 2]), ALU.add), done, loads["rows"], tail_free.get("comp"))
            misc.free(at, z)
            z = put(DVE, "tanh", lambda e: e.tensor_scalar(comp[:, 0], comp[:, 0], 20.0, None, ALU.min), z)
            clusters = calibrate(route[:, :, 0:CL], gate[:, 3], rs, c_read)
            yield next(clusters)
            z = put(ACTE, "tanh_exp", lambda e: e.activation(comp[:, 1], comp[:, 0], ACT.Exp, scale=2.0), z)
            yield next(clusters)
            z = put(DVE, "tanh", lambda e: e.tensor_scalar(comp[:, 1], comp[:, 1], 1.0, None, ALU.add), z)
            z = put(DVE, "tanh", lambda e: e.reciprocal(comp[:, 2], comp[:, 1]), z)
            comp_ready = put(DVE, "tanh", lambda e: e.tensor_scalar(comp[:, 0], comp[:, 2], -2.0, 1.0, ALU.mult, ALU.add), z)

            def first_max(src, dst, ready):
                top = mag[:, :]
                g = put(DVE, "pick", lambda e: e.tensor_reduce(top, src, AX.X, ALU.max), ready)
                g = put(DVE, "pick", lambda e: e.tensor_tensor(
                    src, src, top.unsqueeze(2).broadcast_to([P, NT, CL]), ALU.is_equal), g)
                g = put(DVE, "pick", lambda e: e.tensor_tensor(
                    src, src, rank_row.unsqueeze(1).broadcast_to([P, NT, CL]), ALU.mult), g)
                g = put(DVE, "pick", lambda e: e.tensor_reduce(top, src, AX.X, ALU.max), g)
                return put(DVE, "pick", lambda e: e.tensor_tensor(
                    dst, src, top.unsqueeze(2).broadcast_to([P, NT, CL]), ALU.is_equal), g)

            yield from clusters
            cluster = first_max(gate[:, 3], gate[:, 4], cal[0])
            tiles = route[:, :, CL:].rearrange("p i (c t) -> p i c t", c=CL)
            g = put(DVE, "pick", lambda e: e.tensor_tensor(
                picked_by[:, :, :, :], tiles, gate[:, 4].unsqueeze(3).broadcast_to([P, NT, CL, TPC]), ALU.mult), cluster)
            g = put(DVE, "pick", lambda e: e.tensor_reduce(
                gate[:, 5], picked_by[:, :, :, :].rearrange("p i c t -> p i t c"), AX.X, ALU.add), g)
            yield LATE
            yield from calibrate(gate[:, 5], gate[:, 6], g)
            local = first_max(gate[:, 6], gate[:, 7], cal[0])
            g = put(DVE, "pick", lambda e: e.tensor_tensor(
                picked_by[:, :, :, :], gate[:, 4].unsqueeze(3).broadcast_to([P, NT, CL, TPC]),
                gate[:, 7].unsqueeze(2).broadcast_to([P, NT, CL, TPC]), ALU.mult), local)
            tail_free["route"] = g
            yield LATE
            yield EARLY
            at, ps, free = misc.take()
            for i in range(NT):
                done = put(PE, "pickT" if i == NT - 1 else None, lambda e, i=i, ps=ps: e.transpose(
                    ps[0:TILES, i * P:(i + 1) * P], picked_by[:, i, :, :].rearrange("p c t -> p (c t)"), ident), *free, g)
            picks_read = done
            yield LATE
            pk = put(ACTE, "pickT_done", lambda e, ps=ps: e.activation(pickT, ps[0:TILES, :], ACT.Copy), done, tail_free["p2T"])
            misc.free(at, pk)
            yield EARLY
            directions = buf_d[:, :].rearrange("p (i d) -> p i d", i=NT)
            for i in range(NT):
                at, ps, free = misc.take()
                done = put(PE, "gathered", lambda e, i=i, ps=ps: e.matmul(
                    ps[:, 0:SMALL + D], pickT[:, i * P:(i + 1) * P], table[:, :], start=True, stop=True),
                    *free, pk, *table_ready)
                if i == NT - 1:
                    tail_free["p2T"] = done
                yield LATE
                a1 = put(ACTE, "small", lambda e, i=i, ps=ps: e.activation(small[:, i, :], ps[:, 0:SMALL], ACT.Copy),
                         done, tail_free.get("small"))
                a2 = put(ACTE, "directions", lambda e, i=i, ps=ps: e.activation(
                    directions[:, i, :], ps[:, SMALL:SMALL + D], ACT.Copy), done, d_free)
                misc.free(at, a1, a2)
                yield EARLY if i < NT - 1 else LATE
            h0, h1 = hidden[:, 0], hidden[:, 1]
            by = lambda k: comp[:, 0, :, k:k + 1].broadcast_to([P, NT, GRID])
            g = put(DVE, "spline", lambda e: e.tensor_tensor(h0, small[:, :, 0:GRID], by(0), ALU.mult), a1, comp_ready)
            g2 = put(DVE, "spline", lambda e: e.tensor_tensor(h1, small[:, :, GRID:2 * GRID], by(1), ALU.mult), a1)
            g = put(DVE, "spline", lambda e: e.tensor_tensor(h0, h0, h1, ALU.add), g2)
            g = put(DVE, "spline", lambda e: e.tensor_tensor(h0, h0, small[:, :, 2 * GRID:3 * GRID], ALU.add), g)
            g = put(DVE, "spline", lambda e: e.scalar_tensor_tensor(
                out=h1, in0=h0, scalar=0.0, in1=small[:, :, 3 * GRID:4 * GRID], op0=ALU.max, op1=ALU.mult), g)
            g = put(DVE, "spline", lambda e: e.tensor_reduce(mag[:, :], h1, AX.X, ALU.add), g)
            g = put(DVE, "spline", lambda e: e.tensor_tensor(mag[:, :], mag[:, :], small[:, :, 4 * GRID], ALU.add), g)
            g = put(DVE, "spline", lambda e: e.tensor_scalar(mag[:, :], mag[:, :], out_scale[:, 0:1], None, ALU.mult),
                    g, loads["rows"])
            tail_free["small"] = tail_free["comp"] = g
            tail_free["c"] = [g, picks_read]
            for i in range(NT):
                y = put(DVE, "y", lambda e, i=i: e.scalar_tensor_tensor(
                    out=buf_b[:, i, :], in0=directions[:, i, :], scalar=mag[:, i:i + 1], in1=buf_b[:, i, :],
                    op0=ALU.mult, op1=ALU.add), g, a2)
            tail_free["d"] = y
            yield LATE
            measured, root = measure(buf_b, y)
            yield LATE
            for i in range(NT):
                z = put(DVE, "gamma", lambda e, i=i: e.scalar_tensor_tensor(
                    out=buf_b[:, i, :], in0=buf_b[:, i, :], scalar=moments[:, i, 0:1], in1=gamma[:, :],
                    op0=ALU.subtract, op1=ALU.mult), measured, loads["rows"])
            yield LATE
            for i in range(NT):
                norm_done[0] = put(DVE, "beta", lambda e, i=i: e.scalar_tensor_tensor(
                    out=buf_b[:, i, :], in0=buf_b[:, i, :], scalar=rstd[:, 1, i:i + 1], in1=beta[:, :],
                    op0=ALU.mult, op1=ALU.add), z, root)
            z = norm_done[0]
            for half in range(2):
                stored_half = half_op(half, "x3", buf_b, buf_b, buf_a, ALU.add, z)
                if half == 0:
                    yield LATE
            z = stored_half
            tail_free["a"] = z
            stored[t] = put(SP, "store", lambda e: e.dma_start(
                out[rows, :].rearrange("(i p) d -> p i d", p=P), buf_b[:, :, :]), z, dma=True)

        def run(generator):
            for _ in generator:
                pass

        load("wo", wo[:, :, :], ins["o_wT"].rearrange("(j p) n -> p j n", p=P))
        first, second = prep(0), prep(1)
        for generator, pieces in ((first, 4), (second, 2)):
            for _ in range(pieces):
                next(generator)
        filled = fill_padding()
        run(first)
        split_weights("k", wk_hl, H * HD)
        next(second)
        q_scaled, q_weights = scale_q()
        run(second)
        split_weights("q", wq_hl, 0, q_weights)
        for c in range(PER_BATCH):
            run(project_k(0, 0, c))
        split_weights("v", wv_hl, (H + KV) * HD)

        def setup_tail():
            nonlocal k2_ready, v2_ready, mask_ready, bq2_ready, route_w_ready, temp_ready
            load("wq2", wq2[:, :, :], ins["Wq"].rearrange("(c p) n -> p c n", p=P))
            load("wout2", wout2[:, :, :], ins["Wout"].rearrange("(c p) n -> p c n", p=P))
            wkv = buf_a[:, :, :].rearrange("p a b -> p (a b)").rearrange("p (c n) -> p c n", c=KC)
            load("wkv", wkv, ins["Wkv"].rearrange("(c p) n -> p c n", p=P), x_read[1])
            ctxT = buf_b[:, 0:2, :]
            load("ctxT", ctxT, ins["ctxT"].rearrange("(c p) n -> p c n", p=P))
            mask_words = buf_b[:, 3, HD:2 * HD].bitcast(mybir.dt.uint32)
            mask_u8 = buf_b[:, 3, HD:2 * HD].bitcast(U8)
            load("mask", mask_words, ins["mask"].broadcast_to([P, B * SC // 4]), q_scaled)
            load("sig", buf_c[:, :, 0:TILES], ins["sigT"].rearrange("(c p) n -> p c n", p=P), q_scaled)
            load("cw1", cw1[:, :, :], ins["cw1"].rearrange("(c p) n -> p c n", p=P))
            load("cw2", cw2[:, :], ins["cw2"])
            pad = fill(table[:, :], 0.0)
            parts = (("sw1", 0, 2 * GRID), ("sb1", 2 * GRID, GRID), ("sw2", 3 * GRID, GRID), ("sb2", 4 * GRID, 1),
                     ("directions", SMALL, D))
            for name, at, n in parts:
                table_ready.append(load(name, table[:, at:at + n], ins[name], pad))
            yield LATE
            yield LATE
            bq2_ready = put(DVE, "setup_v", lambda e: e.tensor_scalar(
                bq2[:, :], bq2[:, :], XHD ** -0.5, None, ALU.mult), loads["columns"])
            m = put(DVE, "setup_v", lambda e: e.tensor_copy(mask_add[:, :], mask_u8), loads["mask"])
            mask_ready = put(DVE, "setup_v", lambda e: e.tensor_scalar(
                mask_add[:, :], mask_add[:, :], -3e38, 3.0, ALU.mult, ALU.mult), m)
            yield EARLY
            for m_ in range(KC):
                at, ps, free = misc.take()
                for c in range(KC):
                    done = put(PE, "k2" if c else None, lambda e, m=m_, c=c, ps=ps: e.matmul(
                        ps[:, 0:B * SC], wkv[:, c, m * P:(m + 1) * P], ctxT[:, c, :], start=c == 0, stop=c == 1),
                        *free, loads["wkv"], loads["ctxT"])
                yield LATE
                k2_ready = put(ACTE, "k2T", lambda e, m=m_, ps=ps: e.activation(
                    k2T[:, m, :], ps[:, 0:B * SC], ACT.Identity, bias=bk2[:, m:m + 1]), done, loads["columns"])
                misc.free(at, k2_ready)
                yield EARLY
            for b in range(B):
                at, ps, free = misc.take()
                for hh in range(2):
                    for c in range(KC):
                        done = put(PE, "v2" if c else None, lambda e, b=b, c=c, hh=hh, ps=ps: e.matmul(
                            ps[hh * SC:(hh + 1) * SC, 0:D], ctxT[:, c, b * SC:(b + 1) * SC],
                            wkv[:, c, D:2 * D], start=c == 0, stop=c == 1), *free)
                tail_free["a"] = done
                yield LATE
                for hh in range(2):
                    r = slice(hh * SC, (hh + 1) * SC)
                    v2_ready = put(DVE, "v2_block", lambda e, b=b, hh=hh, r=r, ps=ps: e.tensor_tensor(
                        v2_block[r, b, :, hh, :], ps[r, 0:D].rearrange("p (j a n) -> p j a n", a=2, n=XHD)[:, :, hh, :],
                        bv2[r, :].rearrange("p (j a n) -> p j a n", a=2, n=XHD)[:, :, hh, :], ALU.add),
                        done, loads["setup_rows"], filled)
                misc.free(at, v2_ready)
                yield EARLY if b < B - 1 else LATE
            raw = buf_c[:, :, 0:TILES]
            tern, diff = buf_c[:, :, TILES:2 * TILES], buf_c[:, :, 2 * TILES:3 * TILES]
            g = put(DVE, "sigs", lambda e: e.tensor_scalar(diff, raw, -0.3, None, ALU.is_lt), loads["sig"])
            g2 = put(DVE, "sigs", lambda e: e.tensor_scalar(tern, raw, 0.3, None, ALU.is_gt), loads["sig"])
            g = put(DVE, "sigs", lambda e: e.tensor_tensor(tern, tern, diff, ALU.subtract), g2)
            g = put(DVE, "sigs", lambda e: e.tensor_tensor(diff, tern, raw, ALU.subtract), g)
            sig = route_w[:, :, CL:]
            g = put(DVE, "sigs", lambda e: e.tensor_tensor(sig, raw, diff, ALU.add), g)
            by_tile = sig.rearrange("p k (c t) -> p k t c", c=CL)
            total, negative = buf_c[:, :, 192:192 + CL], buf_c[:, :, 208:208 + CL]
            g = put(DVE, "sigs", lambda e: e.tensor_tensor(total, by_tile[:, :, 0, :], by_tile[:, :, 1, :], ALU.add), g)
            for i in range(2, TPC):
                g = put(DVE, "sigs", lambda e, i=i: e.tensor_tensor(total, total, by_tile[:, :, i, :], ALU.add), g)
            yield LATE
            g = put(DVE, "sigs", lambda e: e.tensor_scalar(negative, total, 0.0, None, ALU.is_lt), g)
            g = put(DVE, "sigs", lambda e: e.tensor_scalar(total, total, 0.0, None, ALU.is_gt), g)
            route_w_ready = put(DVE, "sigs", lambda e: e.tensor_tensor(
                route_w[:, :, 0:CL], total, negative, ALU.subtract), g)
            tail_free["c"] = [route_w_ready]
            g = put(DVE, "setup_v", lambda e: e.tensor_scalar(inv_temp[:, :], temperature, 1e-6, None, ALU.add), loads["rows"])
            g = put(DVE, "setup_v", lambda e: e.reciprocal(mag[:, 0:1], inv_temp[:, :]), g)
            g = put(DVE, "setup_v", lambda e: e.tensor_scalar(inv_temp[:, :], mag[:, 0:1], -1.0, None, ALU.mult), g)
            temp_ready = put(DVE, "setup_v", lambda e: e.tensor_tensor(
                knot_step[:, :], knots[:, 1:KNOTS], knots[:, 0:KNOTS - 1], ALU.subtract), g, loads["rows"])

        k2_ready = v2_ready = mask_ready = bq2_ready = route_w_ready = temp_ready = None
        table_ready = []

        Q_AHEAD, MAX_AHEAD, SHIFT_AHEAD, PV_BEHIND, FINISH_BEHIND = 14, 11, 4, 2, 4
        background = [setup_tail()]
        extra = {}

        def at_step(step, piece):
            extra.setdefault(step, []).append(piece)

        period = PAIRS * KT
        for what, half, first in (("v", 0, -6), ("k", 1, 4), ("v", 1, 8)):
            for c in range(PER_BATCH):
                at_step(first + 2 * c, (what, 0, half, c))
        for b in range(B):
            start = b * PER_BATCH * period
            if b + 1 < B:
                at_step(start + 2 * KT, ("prep", 2 * b + 2))
                at_step(start + 6 * KT, ("prep", 2 * b + 3))
                last = start + (PER_BATCH - 1) * period
                for half in range(2):
                    for c in range(PER_BATCH):
                        at_step(last + (4 * half + 4) * KT + 1 + 2 * c, ("k", b + 1, half, c))
                        at_step(last + (4 * half + 5) * KT + 2 + 2 * c, ("v", b + 1, half, c))
        for t in range(CHUNKS):
            at_step((t + 1) * period + FINISH_BEHIND + 1, ("tail", t))

        units, preps = [], []
        wanted = {}

        def go_on(generators, at, phase):
            if at >= len(generators) or wanted.get(generators[at], EARLY) != phase:
                return False
            wanted[generators[at]] = next(generators[at], None)
            return True

        for step in range(-Q_AHEAD, UNITS * KT + FINISH_BEHIND + 2):
            def unit_at(offset):
                u, r = divmod(step + offset, KT)
                return (u, r) if 0 <= u < UNITS else (None, r)

            u, r = unit_at(Q_AHEAD)
            if u is not None and r == 0:
                units.append(project_q(u))
            u, r = unit_at(SHIFT_AHEAD)
            if u is not None and r == 0:
                units.append(shift_rows(u))
            u, r = unit_at(-(KT - 1) - FINISH_BEHIND)
            if u is not None and r == 0:
                units.append(finish(u))
            for what, *rest in extra.get(step, []):
                if what == "tail":
                    background.append(tail(*rest))
                else:
                    preps.append({"k": project_k, "v": project_v, "prep": prep}[what](*rest))

            u, i = unit_at(MAX_AHEAD)
            if u is not None:
                take_max(u, i)
            crowded = any([go_on(units, at, EARLY) for at in range(len(units))])
            if not go_on(preps, 0, EARLY) and not go_on(background, 0, EARLY) and not crowded:
                go_on(background, 0, ALONE)
            u, kt = unit_at(-PV_BEHIND)
            if u is not None:
                attend(u, kt)
            for at in range(len(units)):
                go_on(units, at, LATE)
            go_on(preps, 0, LATE)
            go_on(background, 0, LATE)
            u, kt = unit_at(0)
            if u is not None:
                score_keys(u, kt)
            for generators in (units, preps, background):
                generators[:] = [g for g in generators if wanted.get(g, EARLY) is not None]
        for generators in (preps, background):
            for generator in generators:
                run(generator)

        last_store = stored[CHUNKS - 1]

        block = ctx.enter_context(nc.Block())

        @block.tensor
        def _(eng):
            q.play(PE, eng)

        @block.scalar
        def _(eng):
            q.play(ACTE, eng)

        @block.vector
        def _(eng):
            q.play(DVE, eng)

        @block.gpsimd
        def _(eng):
            q.play(POOL, eng)

        @block.sync
        def _(eng):
            q.play(SP, eng)
            eng.wait_ge(q.semaphores[last_store[0]], last_store[1])


def kernel(**inputs):
    import numpy as np
    import concourse.bacc as bacc
    from concourse.bass_utils import run_bass_kernel_spmd

    a = {k: np.asarray(v) for k, v in inputs.items()}
    consts = np.zeros((P, P + 16 + HB), np.float32)
    consts[:, 0:P] = np.eye(P)
    consts[:, P:P + 8] = [-1, 1, 2, 3, 4, 5, 6, 100]
    consts[:, P + 8:P + 16] = np.arange(8, 0, -1)
    consts[np.arange(P), P + 16 + np.arange(P) // XHD] = 1
    qkv_b = a["L0_attn_qkv_b"]
    arrays = {
        "x": a["x"].reshape(B * S, D),
        "ctxT": a["ctx_1024"].reshape(B * SC, D).T,
        "mask": a["mask_BxS2_bf0"].reshape(1, B * SC).view(np.uint32),
        "columns": np.concatenate([
            qkv_b[0:H * HD].reshape(PAIRS, P).T, qkv_b[H * HD:(H + KV) * HD].reshape(KV // 2, P).T,
            a["L0_xattn_bq"].reshape(KC, P).T, a["L0_xattn_bkv"][0:D].reshape(KC, P).T,
            np.tile(a["L0_attn_scaling"], 2).reshape(P, 1), np.tile(a["L0_ffn_compress_b1"], 2).reshape(P, 1)], axis=1),
        "rows": np.concatenate([
            qkv_b[(H + KV) * HD:], a["L0_attn_o_b"], a["L0_xattn_bout"], a["L0_ffn_norm_gamma"],
            a["L0_ffn_norm_beta"], a["L0_ffn_compress_b2"], a["L0_ffn_knot_values"], a["L0_ffn_temperature"],
            a["L0_ffn_output_scale"]]).reshape(1, ROWS_N),
        "setup_rows": np.concatenate([a["L0_xattn_bkv"][D:], a["L0_attn_scaling"]]).reshape(1, D + HD),
        "qkv_wT": a["L0_attn_qkv_w"].T,
        "o_wT": a["L0_attn_o_w"].T,
        "Wq": a["L0_xattn_Wq"],
        "Wkv": a["L0_xattn_Wkv"],
        "Wout": a["L0_xattn_Wout"],
        "sigT": a["L0_ffn_signatures_raw"].T,
        "cw1": a["L0_ffn_compress_w1"],
        "cw2": a["L0_ffn_compress_w2"],
        "sw1": a["L0_ffn_spline_w1"].reshape(TILES, 2 * GRID),
        "sb1": a["L0_ffn_spline_b1"],
        "sw2": a["L0_ffn_spline_w2"].reshape(TILES, GRID),
        "sb2": a["L0_ffn_spline_b2"],
        "directions": a["L0_ffn_directions"],
        "consts": consts,
    }
    nc = bacc.Bacc("TRN2", target_bir_lowering=False, num_devices=1)
    in_map, ins = {}, {}
    for name, shape in INPUTS:
        array = np.ascontiguousarray(arrays[name])
        assert array.shape == shape, (name, array.shape)
        in_map[f"in_{name}"] = array
        ins[name] = nc.dram_tensor(f"in_{name}", shape, mybir.dt.from_np(array.dtype), kind="ExternalInput").ap()
    out = nc.dram_tensor("out_x", (B * S, D), F32, kind="ExternalOutput").ap()
    build(nc, ins, out)
    r = run_bass_kernel_spmd(nc, [in_map], core_ids=[0])
    return r.results[0]["out_x"].reshape(B, S, D)
```

```python
from contextlib import ExitStack

import concourse.bass as bass
import numpy as np
from concourse import mybir

F32 = mybir.dt.float32
F32R = mybir.dt.float32r
U8 = mybir.dt.uint8
ALU = mybir.AluOpType
ACT = mybir.ActivationFunctionType
AX = mybir.AxisListType

P = 128
B, S, D = 4, 1024, 256
H, HD, KV = 16, 64, 4
CH = 512
NT = CH // P
CHUNKS = B * S // CH
PER_BATCH = S // CH
KC = D // P
KT = S // P
PAIRS = H // 2
UNITS = CHUNKS * PAIRS
SC = 64
XH = 16
XHD = D // XH
HB = P // XHD
CL, TPC = 8, 8
TILES = CL * TPC
GRID, COMP, KNOTS = 16, 64, 8
SMALL = 4 * GRID + 2
EPS = 1e-5
R_SOFTPLUS_0 = 1.442695041

EARLY, LATE = "early", "late"
ALONE = "alone"

PE, ACTE, DVE, POOL, SP = "tensor", "scalar", "vector", "gpsimd", "sync"

COLUMNS = [("q_bias", PAIRS), ("k_bias", KV // 2), ("bq2", KC), ("bk2", KC), ("scaling", 1), ("cb1", 1)]
ROWS = [("v_bias", KV * HD), ("o_bias", D), ("bout2", D), ("gamma", D), ("beta", D), ("cb2", 2), ("knots", KNOTS),
        ("temperature", 1), ("out_scale", 1)]

ROWS_N = sum(n for _, n in ROWS)

INPUTS = [
    ("columns", (P, sum(n for _, n in COLUMNS))),
    ("rows", (1, sum(n for _, n in ROWS))),
    ("setup_rows", (1, D + HD)),
    ("x", (B * S, D)),
    ("ctxT", (D, B * SC)),
    ("mask", (1, B * SC // 4)),
    ("qkv_wT", (D, (H + 2 * KV) * HD)),
    ("o_wT", (H * HD, D)),
    ("Wq", (D, D)),
    ("Wkv", (D, 2 * D)),
    ("Wout", (D, D)),
    ("sigT", (D, TILES)),
    ("cw1", (D, COMP)),
    ("cw2", (COMP, 2)),
    ("sw1", (TILES, 2 * GRID)),
    ("sb1", (TILES, GRID)),
    ("sw2", (TILES, GRID)),
    ("sb2", (TILES, 1)),
    ("directions", (TILES, D)),
    ("consts", (P, P + 16 + HB)),
]


class Queues:

    def __init__(self, nc, ctx):
        self.nc, self.ctx = nc, ctx
        self.semaphores, self.count = {}, {}
        self.queue = {e: [] for e in (PE, ACTE, DVE, POOL, SP)}
        self.waited = {e: {} for e in self.queue}

    def put(self, engine, stage, instruction, *tokens, dma=False):
        waits = []
        for token in tokens:
            if token is None:
                continue
            name, value = token
            if self.waited[engine].get(name, 0) < value:
                self.waited[engine][name] = value
                waits.append((name, value))
        token = None
        if stage is not None:
            if stage not in self.count:
                self.semaphores[stage] = self.ctx.enter_context(self.nc.semaphore(stage))
                self.count[stage] = 0
            self.count[stage] += 16 if dma else 1
            token = (stage, self.count[stage])
        self.queue[engine].append((waits, instruction, stage, 16 if dma else 1))
        return token

    def play(self, engine, eng):
        for waits, instruction, stage, by in self.queue[engine]:
            for name, value in waits:
                eng.wait_ge(self.semaphores[name], value)
            done = instruction(eng)
            if stage is not None:
                done.then_inc(self.semaphores[stage], by)


class Ring:

    def __init__(self, buffers):
        self.buffers, self.at = buffers, -1
        self.readers = [[] for _ in buffers]

    def take(self):
        self.at = (self.at + 1) % len(self.buffers)
        readers, self.readers[self.at] = self.readers[self.at], None
        assert readers is not None, "a buffer is taken before its readers are known"
        return self.at, self.buffers[self.at], readers

    def free(self, at, *tokens):
        self.readers[at] = list(tokens)


class Workspace:

    def __init__(self, name, nt, first, allocate):
        self.name, self.nt, self.first = name, nt, first
        cols = nt * P

        def new(name, *shape):
            return allocate(name, [P, *shape])

        self.a = new("buf_a", nt, D)
        self.b = new("buf_b", nt, D)
        self.c = new("buf_c", KC, cols)
        self.d = new("buf_d", KC * cols)
        self.weights = Ring([new(f"weights{i}", HB * SC) for i in range(2)])
        self.row_stat = new("row_stat", 3, HB)
        self.p2T = new("p2T", 4, 2 * P)
        self.hT = self.p2T[0:COMP, 0:2, :].rearrange("p a b -> p (a b)")[:, 0:cols]
        self.pickT = self.p2T[0:TILES, 2:4, :].rearrange("p a b -> p (a b)")[:, 0:cols]
        self.route = new("route", nt, CL + TILES)
        self.comp = new("comp", 3, nt, 2)
        self.small = new("small", nt, SMALL)
        words = nt * CL * 8
        flat = self.c[:, :, :].rearrange("p a b -> p (a b)")
        self.gate = flat[:, 0:words].rearrange("p (k i c) -> p k i c", k=8, i=nt)
        self.intervals = flat[:, words:2 * words].rearrange("p (n k) -> p n k", k=KNOTS)
        self.picked_by = flat[:, 2 * words:3 * words].rearrange("p (i c t) -> p i c t", i=nt, c=CL)
        self.hidden = flat[:, 3 * words:3 * words + 2 * nt * GRID].rearrange("p (a i n) -> p a i n", a=2, i=nt)
        self.mag = new("mag", nt)
        self.stats = new("stats", nt, 6)
        self.moments = new("moments", nt, 2)
        self.rstd = new("rstd", 2, nt)
        self.norm_done, self.norm_busy = None, False
        self.free = {"a": None, "c": [], "d": None, "p2T": None}


def build(nc, ins, out):
    with ExitStack() as ctx:
        q = Queues(nc, ctx)
        put = q.put

        pool_done = [None]

        def pool(stage, instruction, *tokens):
            pool_done[0] = put(POOL, stage, instruction, *tokens, pool_done[0])
            return pool_done[0]

        def sb(name, shape, dtype=F32):
            return ctx.enter_context(nc.sbuf_tensor(name, shape, dtype))

        def bank(name, banks=1):
            return ctx.enter_context(nc.psum_tensor(name, [P, banks * 512], F32))

        max_scores = Ring([bank(f"max_scores{i}") for i in range(3)])
        key_scores = Ring([bank(f"key_scores{i}") for i in range(2)])
        attended = bank("attended")
        misc = Ring([bank(f"misc{i}") for i in range(2)])

        consts = sb("consts_sb", [P, P + 16 + HB])
        ident = consts[:, 0:P]
        knot_row = consts[:, P:P + 8]
        rank_row = consts[:, P + 8:P + 16]
        head_block = consts[:, P + 16:P + 16 + HB]
        ones = sb("ones", [P, HD])

        def views(name, parts):
            tile, at, found = sb(name, [P, sum(n for _, n in parts)]), 0, []
            for _, n in parts:
                found.append(tile[:, at:at + n])
                at += n
            return tile, found

        columns, (q_bias, k_bias, bq2, bk2, scaling_column, cb1) = views("columns_sb", COLUMNS)
        rows_sb, (v_bias, o_bias, bout2, gamma, beta, cb2, knots, temperature, out_scale) = views("rows_sb", ROWS)
        minus_half = sb("minus_half", [P, NT])

        wq_hl = sb("wq_hl", [P, 2, KC, H * HD], F32R)
        wk_hl = sb("wk_hl", [P, 2, KC, KV * HD], F32R)
        wv_hl = sb("wv_hl", [P, 2, KC, KV * HD], F32R)
        wo = sb("wo", [P, PAIRS, D])

        x_in = sb("x_in", [P, NT, D])
        xT = Ring([sb(f"xT{i}", [P, 2, KC, CH], F32R) for i in range(3)])
        k_high = sb("k_high", [P, KV, S], F32R)
        k_low = sb("k_low", [P, KV, S], F32R)
        v_all = sb("v_all", [P, KT, KV * HD])
        q_hl = [sb(f"q_hl{i}", [P, 2, CH], F32R) for i in range(3)]
        q_max = [sb(f"q_max{i}", [P, 2, CH], F32R) for i in range(2)]
        minus_max = [sb(f"minus_max{i}", [P, NT, 34]) for i in range(2)]
        probs = Ring([sb(f"probs{i}", [P, CH]) for i in range(6)])
        prob_sum = [sb(f"prob_sum{i}", [P, CH]) for i in range(2)]
        inv_sum = sb("inv_sum", [P, CH])
        raw_out = sb("raw_out", [P, CH])
        heads_out = sb("heads_out", [P, PAIRS, CH])

        wq2 = sb("wq2", [P, KC, D])
        wout2 = sb("wout2", [P, KC, D])
        k2T = sb("k2T", [P, KC, B * SC])
        k2_block = sb("k2_block", [P, KC, HB, SC])
        v2_block = sb("v2_block", [P, B, XH // 2, 2, XHD])
        mask_add = sb("mask_add", [P, B * SC])

        route_w = sb("route_w", [P, KC, CL + TILES])
        cw1 = sb("cw1_sb", [P, KC, COMP])
        cw2 = sb("cw2_sb", [COMP, 2])
        table = sb("table", [TILES, SMALL + D])
        knot_step = sb("knot_step", [P, KNOTS - 1])
        inv_temp = sb("inv_temp", [P, 1])

        main = Workspace("", NT, 0, sb)
        buf_a, buf_b, buf_c, mag = main.a, main.b, main.c, main.mag

        def exp_set():
            put(ACTE, None, lambda e: e.preload_act_table_set("natural_log_exp_and_others"))

        exp_set()
        loads = {}

        def load(name, dst, src, *tokens):
            loads[name] = put(SP, f"load_{name}", lambda e: e.dma_start(dst, src), *tokens, dma=True)
            return loads[name]

        load("consts", consts[:, :], ins["consts"])

        def load_x(t, dst, *tokens):
            rows = ins["x"][t * CH:(t + 1) * CH, :].rearrange("(i p) d -> p i d", p=P)
            return load("x_first" if dst is buf_a else "x_in", dst[:, :, :], rows, *tokens)

        x_loaded = {0: (x_in, load_x(0, x_in)), 1: (buf_a, load_x(1, buf_a))}
        staged = heads_out[:, :, :].rearrange("p a b -> p (a b)")[:, 0:KC * (H + 2 * KV) * HD]
        staged = staged.rearrange("p (c n) -> p c n", c=KC)
        load("qkv_w", staged, ins["qkv_wT"].rearrange("(c p) n -> p c n", p=P))
        load("columns", columns[:, :], ins["columns"])
        load("setup_rows", buf_b[:, 2:4, :].rearrange("p a b -> p (a b)")[:, 0:D + HD], ins["setup_rows"].broadcast_to([P, D + HD]))
        bv2 = buf_b[:, 2, :]
        load("rows", rows_sb[:, :], ins["rows"].broadcast_to([P, ROWS_N]))

        ones_set = put(DVE, "setup_v", lambda e: e.memset(ones[:, :], 1.0))
        def fill(view, value):
            return pool("fills", lambda e: e.memset(view, value))

        half_set = fill(minus_half[:, :], -0.5)

        def fill_padding():
            for i in range(2):
                fill(minus_max[i][:, :, :], 0.0)
                fill(q_max[i][HD:P, :, :].bitcast(F32), 0.0)
            fill(k_low[HD:P, :, :].bitcast(F32), 0.0)
            fill(k_low[HD:HD + 1, :, :].bitcast(F32), 1.0)
            return fill(v2_block[:, :, :, :, :], 0.0)

        split = {}

        def split_weights(name, dst, at, *ready):
            src = staged[:, :, at:at + dst.shape[3]]
            high = put(DVE, "weights_high", lambda e: e.tensor_copy(dst[:, 0], src), loads["qkv_w"], *ready)
            split[name] = put(DVE, "weights_low", lambda e: e.tensor_tensor(
                dst[:, 1], src, dst[:, 0].bitcast(F32), ALU.subtract), high)

        def scale_q():
            def soft(k):
                return buf_c[:, :, :].rearrange("p a b -> p (a b)")[:, k * (HD + 1):(k + 1) * (HD + 1)]

            def vector(instruction, *tokens):
                return put(DVE, "softplus", instruction, *tokens)

            scaling, minus, least, e_, u_, log_u, u1 = [soft(k) for k in range(7)]
            g = vector(lambda e: e.tensor_copy(scaling[:, 0:HD], buf_b[:, 3, 0:HD]), loads["setup_rows"])
            g2 = vector(lambda e: e.tensor_copy(scaling[:, HD:HD + 1], scaling_column), loads["columns"])
            g = vector(lambda e: e.tensor_scalar(minus, scaling, -1.0, None, ALU.mult), g, g2)
            g = vector(lambda e: e.tensor_tensor(least, minus, scaling, ALU.min), g)
            g = put(ACTE, "softplus_exp", lambda e: e.activation(e_, least, ACT.Exp), g)
            g = vector(lambda e: e.tensor_scalar(u_, e_, 1.0, None, ALU.add), g)
            logged = put(ACTE, "softplus_ln", lambda e: e.activation(log_u, u_, ACT.Ln), g)
            rounded = vector(lambda e: e.tensor_scalar(u1, u_, -1.0, None, ALU.add), g)
            g = vector(lambda e: e.tensor_scalar(minus, u1, 1e-30, None, ALU.max), rounded)
            g = vector(lambda e: e.reciprocal(least, minus), g)
            g = vector(lambda e: e.tensor_tensor(minus, least, e_, ALU.mult), g)
            g = vector(lambda e: e.tensor_tensor(minus, minus, log_u, ALU.mult), g, logged)
            g = vector(lambda e: e.tensor_scalar(least, u1, 0.0, None, ALU.is_equal), g)
            g = vector(lambda e: e.tensor_tensor(least, least, e_, ALU.mult), g)
            g = vector(lambda e: e.tensor_tensor(minus, minus, least, ALU.add), g)
            g = vector(lambda e: e.scalar_tensor_tensor(
                out=least, in0=scaling, scalar=0.0, in1=minus, op0=ALU.max, op1=ALU.add), g)
            q_scale = minus
            scaled = vector(lambda e: e.tensor_scalar(q_scale, least, R_SOFTPLUS_0 / HD ** 0.5, None, ALU.mult), g)
            q_scaled = vector(lambda e: e.tensor_scalar(
                q_bias[:, :], q_bias[:, :], q_scale[:, HD:HD + 1], None, ALU.mult), scaled, loads["columns"])

            for c in range(KC):
                wq_scaled = staged[:, c, 0:H * HD].rearrange("p (h d) -> p h d", d=HD)
                q_weights = vector(lambda e, w=wq_scaled: e.tensor_tensor(
                    w, w, q_scale[:, 0:HD].unsqueeze(1).broadcast_to([P, H, HD]), ALU.mult), scaled, loads["qkv_w"])
            return q_scaled, q_weights

        def measure(w, src, *ready):
            tokens = []
            for i in range(w.nt):
                tokens.append(put(DVE, "bn_stats", lambda e, i=i: e.bn_stats(w.stats[:, i, :], src[:, i, :]),
                                  *ready, w.norm_done))
            for i in range(w.nt):
                last = put(DVE, "bn_aggr", lambda e, i=i: e.bn_aggr(w.moments[:, i, :], w.stats[:, i, :]),
                           tokens[i], w.norm_done)
            add = pool("var_eps", lambda e: e.tensor_scalar(
                w.rstd[:, 0, :], w.moments[:, :, 1], EPS, None, ALU.add), last)
            root = pool("rstd", lambda e: e.tensor_tensor(
                w.rstd[:, 1, :], w.rstd[:, 0, :], minus_half[:, 0:w.nt], ALU.pow), add, half_set)
            return last, root

        def layer_norm(w, src, dst, *ready):
            while w.norm_busy:
                yield LATE
            w.norm_busy = True
            _, root = measure(w, src, *ready)
            yield LATE
            for i in range(w.nt):
                w.norm_done = put(DVE, "normed", lambda e, i=i: e.tensor_scalar(
                    dst[:, i, :], src[:, i, :], w.moments[:, i, 0:1], w.rstd[:, 1, i:i + 1],
                    ALU.subtract, ALU.mult), root)
            w.norm_busy = False

        def pair_op(pair, stage, dst, a, b, op, *ready):
            tiles = slice(2 * pair, 2 * pair + 2)
            other = b[:, tiles, :] if len(b.shape) == 3 else b.unsqueeze(1).broadcast_to([P, 2, D])
            return pool(stage, lambda e: e.tensor_tensor(dst[:, tiles, :], a[:, tiles, :], other, op), *ready)

        def transposes(src, nt, c, *ready):
            at, ps, free = misc.take()
            for i in range(nt):
                done = put(PE, "x_transposed" if i == nt - 1 else None, lambda e, i=i: e.transpose(
                    ps[:, i * P:(i + 1) * P], src[:, i, c * P:(c + 1) * P], ident), *ready, *free, loads["consts"])
            return at, ps, done

        x_ready, x_slot = {}, {}
        x_read = {}
        xT_readers = {}

        def prep(t):
            x_in, loaded = x_loaded[t]
            yield LATE
            yield from layer_norm(main, x_in, x_in, loaded)
            yield LATE
            yield EARLY
            slot, buf, free = xT.take()
            x_slot[t] = (slot, buf)
            xT_readers[t] = []
            for c in range(KC):
                at, ps, done = transposes(x_in, NT, c, main.norm_done)
                yield LATE
                high = put(ACTE, "xT_high", lambda e, ps=ps, c=c: e.activation(buf[:, 0, c, :], ps[:, :], ACT.Copy), done, *free)
                low = put(DVE, "xT_low", lambda e, ps=ps, c=c: e.tensor_tensor(
                    buf[:, 1, c, :], ps[:, :], buf[:, 0, c, :].bitcast(F32), ALU.subtract), done, high, *free)
                misc.free(at, low)
                if c < KC - 1:
                    yield EARLY
            x_ready[t] = low
            x_read[t] = done
            follower = t + 1 if t else 2
            if t != 1 and follower < CHUNKS:
                x_loaded[follower] = x_in, load_x(follower, x_in, done)

        def three_products(ps_out, lhs, rhs, stage, *ready):
            terms = [(a, b, c) for c in range(KC) for a, b in ((0, 0), (0, 1), (1, 0))]
            for n, (a, b, c) in enumerate(terms):
                token = put(PE, stage if n == len(terms) - 1 else None, lambda e, a=a, b=b, c=c, n=n: e.matmul(
                    ps_out, lhs(a, c), rhs(b, c), start=n == 0, stop=n == len(terms) - 1), *ready)
            return token

        k_ready, v_ready = {}, {}
        k_read, v_read = {}, {}

        def project_k(b, half, c):
            t = b * PER_BATCH + c
            _, buf = x_slot[t]
            at, ps, free = misc.take()
            done = three_products(ps[:, :], lambda a, kc: wk_hl[:, a, kc, half * P:(half + 1) * P],
                                  lambda a, kc: buf[:, a, kc, :], "k_projected", *free, x_ready[t], split["k"])
            xT_readers[t].append(done)
            yield LATE
            cols = slice(c * CH, (c + 1) * CH)
            for head in range(2):
                g = 2 * half + head
                rows = slice(head * HD, (head + 1) * HD)
                for copy in range(2):
                    high = put(ACTE, "k_high", lambda e, g=g, r=rows, o=copy * HD: e.activation(
                        k_high[o:o + HD, g, cols], ps[r, :], ACT.Identity, bias=k_bias[r, half:half + 1]),
                        done, k_read.get(g), loads["columns"])
                low = put(DVE, "k_low", lambda e, g=g, r=rows: e.scalar_tensor_tensor(
                    out=k_low[0:HD, g, cols], in0=ps[r, :], scalar=k_bias[r, half:half + 1],
                    in1=k_high[r, g, cols].bitcast(F32), op0=ALU.add, op1=ALU.subtract), high)
                k_ready[b, g, c] = low
            misc.free(at, low)

        def project_v(b, half, c):
            t = b * PER_BATCH + c
            _, buf = x_slot[t]
            at, ps, free = misc.take()
            n = KV // 2 * HD
            for i in range(NT):
                done = three_products(
                    ps[:, i * n:(i + 1) * n], lambda a, kc, i=i: buf[:, a, kc, i * P:(i + 1) * P],
                    lambda a, kc: wv_hl[:, a, kc, half * n:(half + 1) * n], "v_projected", *free,
                    x_ready[t], split["v"])
            xT_readers[t].append(done)
            yield LATE
            token = put(DVE, "v_all", lambda e: e.tensor_tensor(
                v_all[:, c * NT:(c + 1) * NT, half * n:(half + 1) * n],
                ps[:, :].rearrange("p (i n) -> p i n", i=NT),
                v_bias[:, half * n:(half + 1) * n].unsqueeze(1).broadcast_to([P, NT, n]), ALU.add),
                done, loads["rows"], v_read.get(half))
            misc.free(at, token)
            v_ready[b, half, c] = token

        q_hl_ready, q_max_ready = {}, {}
        pass2_done, max_taken, shift_done = {}, {}, {}
        exps = {}
        sum_done = {}
        attended_free = [None]
        heads_ready = {}
        heads_read = {}

        def project_q(u):
            t, p = divmod(u, PAIRS)
            slot, buf = x_slot[t]
            dst = q_hl[u % 3]
            at, ps, free = misc.take()
            done = three_products(ps[:, :], lambda a, kc: wq_hl[:, a, kc, p * P:(p + 1) * P],
                                  lambda a, kc: buf[:, a, kc, :], "q_projected", *free, x_ready[t], split["q"])
            xT_readers[t].append(done)
            if p == PAIRS - 1:
                xT.free(slot, *xT_readers[t])
            yield LATE
            old = pass2_done.get(u - 3)
            for head in range(2):
                rows, other = slice(head * HD, (head + 1) * HD), slice((1 - head) * HD, (2 - head) * HD)
                high = put(ACTE, "q_high", lambda e, r=rows, h=head: e.activation(
                    dst[r, h, :], ps[r, :], ACT.Identity, bias=q_bias[r, p:p + 1]), done, q_scaled, old)
                low = put(DVE, "q_low", lambda e, r=rows, o=other, h=head: e.scalar_tensor_tensor(
                    out=dst[o, h, :], in0=ps[r, :], scalar=q_bias[r, p:p + 1], in1=dst[r, h, :].bitcast(F32),
                    op0=ALU.add, op1=ALU.subtract), high)
            misc.free(at, low)
            q_hl_ready[u] = low

        def take_max(u, i):
            t, p = divmod(u, PAIRS)
            b, g = t // PER_BATCH, p // 2
            head, tile = divmod(i, NT)
            src, dst = q_hl[u % 3], minus_max[u % 2]
            for half in range(2):
                at, ps, free = max_scores.take()
                done = put(PE, "max_scores", lambda e, half=half, ps=ps: e.matmul(
                    ps[:, :], src[:, head, tile * P:(tile + 1) * P],
                    k_high[:, g, half * 512:(half + 1) * 512], start=True, stop=True),
                    q_hl_ready[u], k_ready[b, g, 0], k_ready[b, g, 1], *free)
                column = 32 * head + half
                token = put(DVE, "minus_max", lambda e, c=column, ps=ps: e.tensor_reduce(
                    dst[:, tile, c:c + 1], ps[:, :], AX.X, ALU.max, negate=True),
                    done, shift_done.get(u - 2), filled)
                max_scores.free(at, token)
            if i == 2 * NT - 1:
                max_taken[u] = put(DVE, "both_halves", lambda e: e.tensor_tensor(
                    dst[:, :, 0::32], dst[:, :, 0::32], dst[:, :, 1::32], ALU.min), token)

        def shift_rows(u):
            src, high, dst = minus_max[u % 2], q_hl[u % 3], q_max[u % 2]
            old = pass2_done.get(u - 2)
            for head in range(2):
                yield LATE
                rows = slice(head * HD, (head + 1) * HD)
                again = pool("q_high_again", lambda e, h=head, r=rows: e.tensor_copy(
                    dst[0:HD, h, :], high[r, h, :].bitcast(F32)), q_hl_ready[u], old)
            yield EARLY
            at, ps, free = misc.take()
            for i in range(NT):
                done = put(PE, "max_transposed" if i == NT - 1 else None, lambda e, i=i: e.transpose(
                    ps[0:34, i * P:(i + 1) * P], src[:, i, :], ident), max_taken[u], *free, loads["consts"])
            shift_done[u] = done
            yield LATE
            tokens = [again]
            for head in range(2):
                tokens.append(put(ACTE, "max_row", lambda e, h=head: e.activation(
                    dst[HD:HD + 1, h, :], ps[32 * h:32 * h + 1, :], ACT.Copy), done, old, filled))
            misc.free(at, tokens[-1])
            q_max_ready[u] = tokens

        def score_keys(u, kt):
            t, p = divmod(u, PAIRS)
            b, g = t // PER_BATCH, p // 2
            high, shifted = q_hl[u % 3], q_max[u % 2]
            keys = slice(kt * P, (kt + 1) * P)
            for head in range(2):
                at, ps, free = key_scores.take()
                put(PE, None, lambda e, h=head, ps=ps: e.matmul(
                    ps[:, :], k_high[:, g, keys], high[:, h, :], start=True, stop=False), *free,
                    q_hl_ready[u], k_ready[b, g, 0], k_ready[b, g, 1])
                done = put(PE, "key_scores", lambda e, h=head, ps=ps: e.matmul(
                    ps[:, :], k_low[:, g, keys], shifted[:, h, :], start=False, stop=True),
                    *q_max_ready[u], filled)
                slot, buf, readers = probs.take()
                token = put(ACTE, "exp", lambda e, ps=ps, buf=buf: e.activation(buf[:, :], ps[:, :], ACT.Exp),
                            done, *readers)
                key_scores.free(at, token)
                exps[u, kt, head] = (slot, buf, token)
            pass2_done[u] = done
            k_read[g] = done

        def attend(u, kt):
            t, p = divmod(u, PAIRS)
            b, half = t // PER_BATCH, p // 4
            g = p // 2
            pv = []
            for head in range(2):
                slot, buf, token = exps[u, kt, head]
                pv.append(put(PE, "attended", lambda e, h=head, buf=buf: e.matmul(
                    attended[h * HD:(h + 1) * HD, :], v_all[:, kt, g * HD:(g + 1) * HD], buf[:, :],
                    start=kt == 0, stop=kt == KT - 1), token, v_ready[b, half, 0], v_ready[b, half, 1],
                    attended_free[0] if kt == 0 else None))
            v_read[half] = pv[1]
            if kt == KT - 1:
                attended_free[0] = put(ACTE, "raw_out", lambda e: e.activation(
                    raw_out[:, :], attended[:, :], ACT.Copy), pv[1], heads_ready.get(u - 1))
            if kt == 0:
                return
            for head in range(2):
                add = (lambda *a: put(DVE, *a), pool)[head]
                slot, buf, token = exps[u, kt, head]
                acc = prob_sum[head]
                if kt == 1:
                    first_slot, first, first_token = exps[u, 0, head]
                    done = add(f"prob_sum{head}", lambda e, a=acc, x=first, y=buf: e.tensor_tensor(
                        a[:, :], x[:, :], y[:, :], ALU.add), first_token, token, sum_done.get(u - 1))
                    probs.free(first_slot, done, pv[head])
                else:
                    done = add(f"prob_sum{head}", lambda e, a=acc, y=buf: e.tensor_tensor(
                        a[:, :], a[:, :], y[:, :], ALU.add), token, sum_token[head])
                sum_token[head] = done
                probs.free(slot, done, pv[head])

        sum_token = [None, None]

        def finish(u):
            t, p = divmod(u, PAIRS)
            at, ps, free = misc.take()
            for head in range(2):
                done = put(PE, "sums", lambda e, h=head: e.matmul(
                    ps[h * HD:(h + 1) * HD, :], ones[:, :], prob_sum[h][:, :], start=True, stop=True),
                    sum_token[head], *free, ones_set)
            sum_done[u] = done
            yield LATE
            ln = put(ACTE, "ln_sum", lambda e: e.activation(inv_sum[:, :], ps[:, :], ACT.Ln), done, heads_ready.get(u - 1))
            misc.free(at, ln)
            inv = put(ACTE, "inv_sum", lambda e: e.activation(inv_sum[:, :], inv_sum[:, :], ACT.Exp, scale=-1.0), ln)
            yield LATE
            token = pool("heads_out", lambda e: e.tensor_tensor(
                heads_out[:, p, :], raw_out[:, :], inv_sum[:, :], ALU.mult), attended_free[0], inv, heads_read.get(p), split["v"])
            heads_ready[u] = token

        context_keys = {"ready": None, "read": None}
        stores = []

        def tail(t, w):
            b = t // PER_BATCH
            nt, cols = w.nt, w.nt * P
            weights, row_stat, p2T, hT, pickT, route, comp, small, mag = (
                w.weights, w.row_stat, w.p2T, w.hT, w.pickT, w.route, w.comp, w.small, w.mag)
            buf_a, buf_b, buf_c, buf_d = w.a, w.b, w.c, w.d
            gate, intervals, picked_by, hidden = w.gate, w.intervals, w.picked_by, w.hidden
            start = t * CH + w.first * P
            rows = slice(start, start + cols)
            x_rows = ins["x"][rows, :].rearrange("(i p) d -> p i d", p=P)
            xl = load(f"residual{w.name}", buf_a[:, :, :], x_rows, w.free.get("b"), w.free["a"])
            yield EARLY
            for i in range(nt):
                at, ps, free = misc.take()
                for p in range(PAIRS):
                    done = put(PE, "projected" if p == PAIRS - 1 else None, lambda e, p=p, i=i, ps=ps: e.matmul(
                        ps[:, 0:D], heads_out[:, p, (w.first + i) * P:(w.first + i + 1) * P], wo[:, p, :], start=p == 0, stop=p == PAIRS - 1),
                        *free, heads_ready[t * PAIRS + p], loads["wo"])
                if i == nt - 1:
                    for p in range(PAIRS):
                        heads_read[p] = done
                yield LATE
                if i < nt // 2:
                    biased = pair_op(i, "residual_bias", buf_a, buf_a, o_bias[:, :], ALU.add, xl, loads["rows"])
                x1 = put(DVE, "x1", lambda e, i=i, ps=ps: e.tensor_tensor(
                    buf_a[:, i, :], ps[:, 0:D], buf_a[:, i, :], ALU.add), done, biased)
                misc.free(at, x1)
                yield EARLY if i < nt - 1 else LATE
            yield from layer_norm(w, buf_a, buf_b, x1, w.free.get("b"))
            normed = w.norm_done
            yield EARLY
            for c in range(KC):
                at, ps, done = transposes(buf_b, nt, c, normed)
                yield LATE
                if c < nt // 2:
                    a_bias = pair_op(c, "output_bias", buf_a, buf_a, bout2[:, :], ALU.add, normed, loads["rows"])
                ct = put(ACTE, "normT", lambda e, c=c, ps=ps: e.activation(buf_c[:, c, :], ps[:, 0:cols], ACT.Copy),
                         done, *w.free["c"])
                misc.free(at, ct)
                yield EARLY
            if t % PER_BATCH == 0:
                for m in range(KC):
                    k2_done = pool("k2_block", lambda e, m=m: e.tensor_tensor(
                        k2_block[:, m, :, :], k2T[:, m, b * SC:(b + 1) * SC].unsqueeze(1).broadcast_to([P, HB, SC]),
                        head_block.unsqueeze(2).broadcast_to([P, HB, SC]), ALU.mult),
                        k2_ready, context_keys["read"])
                context_keys["ready"] = k2_done
            k2_done = context_keys["ready"]
            for m in range(KC):
                at, ps, free = misc.take()
                for c in range(KC):
                    done = put(PE, "q2" if c else None, lambda e, m=m, c=c, ps=ps: e.matmul(
                        ps[:, 0:cols], wq2[:, c, m * P:(m + 1) * P], buf_c[:, c, :], start=c == 0, stop=c == 1),
                        *free, ct, loads["wq2"])
                yield LATE
                qd = put(ACTE, "q2_done", lambda e, m=m, ps=ps: e.activation(
                    buf_d[:, m * cols:(m + 1) * cols], ps[:, 0:cols], ACT.Identity, scale=XHD ** -0.5, bias=bq2[:, m:m + 1]),
                    done, bq2_ready, w.free["d"])
                misc.free(at, qd)
                yield EARLY
            w.free["c"] = [done]
            tiles = [(m, i) for m in range(KC) for i in range(nt)]
            p2_free = w.free["p2T"]
            soft, normal = {}, {}
            for n in range(len(tiles) + 2):
                if n < len(tiles):
                    m, i = tiles[n]
                    at, ps, free = misc.take()
                    scored = put(PE, "scores2", lambda e, m=m, i=i, ps=ps: e.matmul(
                        ps[:, :], buf_d[:, m * cols + i * P:m * cols + (i + 1) * P],
                        k2_block[:, m, :, :].rearrange("p a b -> p (a b)"), start=True, stop=True),
                        *free, qd, k2_done)
                pair_done = n >= 3 and n % 2 == 1
                if pair_done:
                    m, i = tiles[n - 3]
                    at2, ps2, free = misc.take()
                    for j in range(4):
                        done = put(PE, "attended2", lambda e, j=j, m=m, ps=ps2: e.matmul(
                            ps[32 * j:32 * j + 32, 0:2 * P],
                            v2_block[:, b, 4 * m + j, :, :].rearrange("p a b -> p (a b)"), p2T[:, j, :],
                            start=True, stop=True), *free, ev, v2_ready)
                    p2_free = done
                if n != len(tiles):
                    yield LATE
                if pair_done:
                    ot = put(ACTE, "out2T", lambda e, m=m, i=i, ps=ps2: e.activation(
                        buf_d[:, m * cols + i * P:m * cols + (i + 2) * P], ps[:, 0:2 * P], ACT.Copy), done)
                    misc.free(at2, ot)
                if n < len(tiles):
                    slot, probs2, w_free = weights.take()
                    w3 = probs2[:, :].rearrange("p (h k) -> p h k", h=HB)
                    s = put(DVE, "soft2", lambda e, ps=ps, w3=w3: e.tensor_tensor(
                        w3, ps[:, :].rearrange("p (h k) -> p h k", h=HB),
                        mask_add[:, b * SC:(b + 1) * SC].unsqueeze(1).broadcast_to([P, HB, SC]), ALU.add),
                        scored, mask_ready, *w_free)
                    misc.free(at, s)
                    mx = put(DVE, "soft2", lambda e, w3=w3: e.tensor_reduce(
                        row_stat[:, 0, :], w3, AX.X, ALU.max), s, q_scaled)
                    less = put(DVE, "soft2", lambda e, w3=w3: e.tensor_tensor(
                        w3, w3, row_stat[:, 0, :].unsqueeze(2).broadcast_to([P, HB, SC]), ALU.subtract), mx)
                    soft[n] = (slot, probs2, w3)
                if n > len(tiles):
                    break
                if n < len(tiles):
                    yield EARLY
                    ex = put(ACTE, "exp2", lambda e, probs2=probs2: e.activation(probs2[:, :], probs2[:, :], ACT.Exp), less)
                transposing = 1 <= n <= len(tiles)
                if transposing:
                    _, i = tiles[n - 1]
                    before, probs2, _ = soft[n - 1]
                    at, ps, free = misc.take()
                    for j in range(4):
                        done = put(PE, "weights2T" if j == 3 else None, lambda e, j=j, probs2=probs2, ps=ps: e.transpose(
                            ps[:, j * P:(j + 1) * P], probs2[:, j * P:(j + 1) * P], ident), *free, normal[n - 1])
                    weights.free(before, done)
                yield LATE
                if transposing:
                    ev = put(ACTE, "p2T", lambda e, i=i, ps=ps: e.activation(
                        p2T[:, :, (i % 2) * P:(i % 2 + 1) * P], ps[:, :].rearrange("p (j n) -> p j n", j=4), ACT.Copy),
                        done, p2_free)
                    misc.free(at, ev)
                if n < len(tiles):
                    _, _, w3 = soft[n]
                    sm = put(DVE, "soft2", lambda e, w3=w3: e.tensor_reduce(
                        row_stat[:, 1, :], w3, AX.X, ALU.add), ex)
                    sm = put(DVE, "soft2", lambda e: e.reciprocal(row_stat[:, 2, :], row_stat[:, 1, :]), sm, w.free.get("rs"))
                    normal[n] = w.free["rs"] = pool("weights2", lambda e, w3=w3: e.tensor_tensor(
                        w3, w3, row_stat[:, 2, :].unsqueeze(2).broadcast_to([P, HB, SC]), ALU.mult), sm)
                yield ALONE if n >= 2 and n % 2 == 0 and n < len(tiles) else EARLY
            yield EARLY
            context_keys["read"] = done
            w.free["p2T"] = done
            for pair in range(nt // 2):
                at, ps, free = misc.take()
                for i in range(2):
                    for m in range(KC):
                        col = m * cols + (2 * pair + i) * P
                        done = put(PE, "projected2" if m else None, lambda e, m=m, i=i, col=col, ps=ps: e.matmul(
                            ps[:, i * D:(i + 1) * D], buf_d[:, col:col + P], wout2[:, m, :],
                            start=m == 0, stop=m == 1), *free, ot, loads["wout2"])
                yield LATE
                tile_pair = buf_a[:, 2 * pair:2 * pair + 2, :]
                x2 = put(DVE, "x2", lambda e, dst=tile_pair, ps=ps: e.tensor_tensor(
                    dst, ps[:, :].rearrange("p (i d) -> p i d", i=2), dst, ALU.add), done, a_bias)
                misc.free(at, x2)
                yield EARLY if pair == 0 else LATE
            d_free = done
            yield from layer_norm(w, buf_a, buf_b, x2)
            normed = w.norm_done
            yield LATE
            yield EARLY
            for c in range(KC):
                at, ps, done = transposes(buf_b, nt, c, normed)
                yield LATE
                ct = put(ACTE, "normT", lambda e, c=c, ps=ps: e.activation(buf_c[:, c, :], ps[:, 0:cols], ACT.Copy),
                         done, *w.free["c"])
                misc.free(at, ct)
                yield EARLY
            at, ps, free = misc.take()
            n = CL + TILES
            for i in range(nt):
                for c in range(KC):
                    done = put(PE, "route_scores" if c else None, lambda e, i=i, c=c, ps=ps: e.matmul(
                        ps[:, i * n:(i + 1) * n], buf_c[:, c, i * P:(i + 1) * P], route_w[:, c, :],
                        start=c == 0, stop=c == 1), *free, ct, route_w_ready)
            yield LATE
            rs = put(ACTE, "route", lambda e, ps=ps: e.activation(
                route[:, :, :], ps[:, 0:nt * n].rearrange("p (i n) -> p i n", i=nt), ACT.Copy), done, w.free.get("route"))
            misc.free(at, rs)
            yield EARLY
            at, ps, free = misc.take()
            for c in range(KC):
                done = put(PE, "compressed" if c else None, lambda e, c=c, ps=ps: e.matmul(
                    ps[0:COMP, 0:cols], cw1[:, c, :], buf_c[:, c, :], start=c == 0, stop=c == 1), *free, loads["cw1"])
            c_read = done
            yield LATE
            ge = put(ACTE, "gelu", lambda e, ps=ps: e.activation(
                hT, ps[0:COMP, 0:cols], ACT.Gelu, bias=cb1[0:COMP, 0:1]), done, loads["columns"], w.free["p2T"])
            exp_set()
            misc.free(at, ge)
            yield EARLY
            at, ps, free = misc.take()
            for i in range(nt):
                done = put(PE, "comp" if i == nt - 1 else None, lambda e, i=i, ps=ps: e.matmul(
                    ps[:, 2 * i:2 * i + 2], hT[:, i * P:(i + 1) * P], cw2[:, :], start=True, stop=True),
                    *free, ge, loads["cw2"])
            yield LATE
            cal = [None]

            def calibrate(src, dst, *ready):
                flat = lambda k: gate[:, k].rearrange("p a b -> p (a b)")
                g = put(DVE, "gate", lambda e: e.tensor_scalar(
                    gate[:, 0], src, inv_temp[:, 0:1], 88.0, ALU.mult, ALU.min), *ready, temp_ready)
                yield EARLY
                g = put(ACTE, "gate_exp", lambda e: e.activation(gate[:, 0], gate[:, 0], ACT.Exp), g)
                yield LATE
                g = put(DVE, "gate", lambda e: e.tensor_scalar(gate[:, 0], gate[:, 0], 1.0, None, ALU.add), g)
                g = put(DVE, "gate", lambda e: e.reciprocal(gate[:, 1], gate[:, 0]), g)
                f = put(DVE, "gate", lambda e: e.tensor_scalar(gate[:, 0], gate[:, 1], KNOTS - 1.0, None, ALU.mult), g)
                g = put(DVE, "gate", lambda e: e.tensor_tensor(
                    intervals[:, :, :], flat(0).unsqueeze(2).broadcast_to([P, nt * CL, KNOTS]),
                    knot_row.unsqueeze(1).broadcast_to([P, nt * CL, KNOTS]), ALU.is_ge), f)
                low = put(DVE, "gate", lambda e: e.tensor_reduce(
                    flat(1), intervals[:, :, 1:KNOTS], AX.X, ALU.add), g)
                t_ = put(DVE, "gate", lambda e: e.tensor_tensor(gate[:, 0], gate[:, 0], gate[:, 1], ALU.subtract), low)
                yield LATE
                one = put(DVE, "gate", lambda e: e.tensor_tensor(
                    intervals[:, :, 0:KNOTS - 1], intervals[:, :, 0:KNOTS - 1], intervals[:, :, 1:KNOTS],
                    ALU.subtract), t_)
                for k, values in ((1, knots[:, 0:KNOTS - 1]), (2, knot_step[:, :])):
                    pick = put(DVE, "gate", lambda e, values=values: e.tensor_tensor(
                        picked(values), intervals[:, :, 0:KNOTS - 1],
                        values.unsqueeze(1).broadcast_to([P, nt * CL, KNOTS - 1]), ALU.mult), one, temp_ready)
                    one = put(DVE, "gate", lambda e, k=k: e.tensor_reduce(flat(k), picked(None), AX.X, ALU.add), pick)
                g = put(DVE, "gate", lambda e: e.tensor_tensor(gate[:, 0], gate[:, 0], gate[:, 2], ALU.mult), one)
                cal[0] = put(DVE, "gate", lambda e: e.tensor_tensor(dst, gate[:, 0], gate[:, 1], ALU.add), g)

            def picked(_):
                return picked_by[:, :, :, :].rearrange("p a b c -> p (a b) c")[:, :, 0:KNOTS - 1]

            z = put(DVE, "tanh", lambda e, ps=ps: e.tensor_tensor(
                comp[:, 0], ps[:, 0:2 * nt].rearrange("p (i n) -> p i n", i=nt),
                cb2[:, :].unsqueeze(1).broadcast_to([P, nt, 2]), ALU.add), done, loads["rows"], w.free.get("comp"))
            misc.free(at, z)
            z = put(DVE, "tanh", lambda e: e.tensor_scalar(comp[:, 0], comp[:, 0], 20.0, None, ALU.min), z)
            clusters = calibrate(route[:, :, 0:CL], gate[:, 3], rs, c_read)
            yield next(clusters)
            z = put(ACTE, "tanh_exp", lambda e: e.activation(comp[:, 1], comp[:, 0], ACT.Exp, scale=2.0), z)
            yield next(clusters)
            z = put(DVE, "tanh", lambda e: e.tensor_scalar(comp[:, 1], comp[:, 1], 1.0, None, ALU.add), z)
            z = put(DVE, "tanh", lambda e: e.reciprocal(comp[:, 2], comp[:, 1]), z)
            comp_ready = put(DVE, "tanh", lambda e: e.tensor_scalar(comp[:, 0], comp[:, 2], -2.0, 1.0, ALU.mult, ALU.add), z)

            def first_max(src, dst, ready):
                top = mag[:, :]
                g = put(DVE, "pick", lambda e: e.tensor_reduce(top, src, AX.X, ALU.max), ready)
                g = put(DVE, "pick", lambda e: e.tensor_tensor(
                    src, src, top.unsqueeze(2).broadcast_to([P, nt, CL]), ALU.is_equal), g)
                g = put(DVE, "pick", lambda e: e.tensor_tensor(
                    src, src, rank_row.unsqueeze(1).broadcast_to([P, nt, CL]), ALU.mult), g)
                g = put(DVE, "pick", lambda e: e.tensor_reduce(top, src, AX.X, ALU.max), g)
                return put(DVE, "pick", lambda e: e.tensor_tensor(
                    dst, src, top.unsqueeze(2).broadcast_to([P, nt, CL]), ALU.is_equal), g)

            yield from clusters
            cluster = first_max(gate[:, 3], gate[:, 4], cal[0])
            tiles = route[:, :, CL:].rearrange("p i (c t) -> p i c t", c=CL)
            g = put(DVE, "pick", lambda e: e.tensor_tensor(
                picked_by[:, :, :, :], tiles, gate[:, 4].unsqueeze(3).broadcast_to([P, nt, CL, TPC]), ALU.mult), cluster)
            g = put(DVE, "pick", lambda e: e.tensor_reduce(
                gate[:, 5], picked_by[:, :, :, :].rearrange("p i c t -> p i t c"), AX.X, ALU.add), g)
            yield LATE
            yield from calibrate(gate[:, 5], gate[:, 6], g)
            local = first_max(gate[:, 6], gate[:, 7], cal[0])
            g = put(DVE, "pick", lambda e: e.tensor_tensor(
                picked_by[:, :, :, :], gate[:, 4].unsqueeze(3).broadcast_to([P, nt, CL, TPC]),
                gate[:, 7].unsqueeze(2).broadcast_to([P, nt, CL, TPC]), ALU.mult), local)
            w.free["route"] = g
            yield LATE
            yield EARLY
            at, ps, free = misc.take()
            for i in range(nt):
                done = put(PE, "pickT" if i == nt - 1 else None, lambda e, i=i, ps=ps: e.transpose(
                    ps[0:TILES, i * P:(i + 1) * P], picked_by[:, i, :, :].rearrange("p c t -> p (c t)"), ident), *free, g)
            picks_read = done
            yield LATE
            pk = put(ACTE, "pickT_done", lambda e, ps=ps: e.activation(pickT, ps[0:TILES, 0:cols], ACT.Copy), done, w.free["p2T"])
            misc.free(at, pk)
            yield EARLY
            directions = buf_d[:, :].rearrange("p (i d) -> p i d", i=nt)
            for i in range(nt):
                at, ps, free = misc.take()
                done = put(PE, "gathered", lambda e, i=i, ps=ps: e.matmul(
                    ps[:, 0:SMALL + D], pickT[:, i * P:(i + 1) * P], table[:, :], start=True, stop=True),
                    *free, pk, *table_ready)
                if i == nt - 1:
                    w.free["p2T"] = done
                yield LATE
                a1 = put(ACTE, "small", lambda e, i=i, ps=ps: e.activation(small[:, i, :], ps[:, 0:SMALL], ACT.Copy),
                         done, w.free.get("small"))
                a2 = put(ACTE, "directions", lambda e, i=i, ps=ps: e.activation(
                    directions[:, i, :], ps[:, SMALL:SMALL + D], ACT.Copy), done, d_free)
                misc.free(at, a1, a2)
                yield EARLY if i < nt - 1 else LATE
            h0, h1 = hidden[:, 0], hidden[:, 1]
            by = lambda k: comp[:, 0, :, k:k + 1].broadcast_to([P, nt, GRID])
            g = put(DVE, "spline", lambda e: e.tensor_tensor(h0, small[:, :, 0:GRID], by(0), ALU.mult), a1, comp_ready)
            g2 = put(DVE, "spline", lambda e: e.tensor_tensor(h1, small[:, :, GRID:2 * GRID], by(1), ALU.mult), a1)
            g = put(DVE, "spline", lambda e: e.tensor_tensor(h0, h0, h1, ALU.add), g2)
            g = put(DVE, "spline", lambda e: e.tensor_tensor(h0, h0, small[:, :, 2 * GRID:3 * GRID], ALU.add), g)
            g = put(DVE, "spline", lambda e: e.scalar_tensor_tensor(
                out=h1, in0=h0, scalar=0.0, in1=small[:, :, 3 * GRID:4 * GRID], op0=ALU.max, op1=ALU.mult), g)
            g = put(DVE, "spline", lambda e: e.tensor_reduce(mag[:, :], h1, AX.X, ALU.add), g)
            g = put(DVE, "spline", lambda e: e.tensor_tensor(mag[:, :], mag[:, :], small[:, :, 4 * GRID], ALU.add), g)
            g = put(DVE, "spline", lambda e: e.tensor_scalar(mag[:, :], mag[:, :], out_scale[:, 0:1], None, ALU.mult),
                    g, loads["rows"])
            w.free["small"] = w.free["comp"] = g
            w.free["c"] = [g, picks_read]
            for i in range(nt):
                y = put(DVE, "y", lambda e, i=i: e.scalar_tensor_tensor(
                    out=buf_b[:, i, :], in0=directions[:, i, :], scalar=mag[:, i:i + 1], in1=buf_b[:, i, :],
                    op0=ALU.mult, op1=ALU.add), g, a2)
            w.free["d"] = y
            yield LATE
            while w.norm_busy:
                yield LATE
            w.norm_busy = True
            measured, root = measure(w, buf_b, y)
            yield LATE
            for i in range(nt):
                z = put(DVE, "gamma", lambda e, i=i: e.scalar_tensor_tensor(
                    out=buf_b[:, i, :], in0=buf_b[:, i, :], scalar=w.moments[:, i, 0:1], in1=gamma[:, :],
                    op0=ALU.subtract, op1=ALU.mult), measured, loads["rows"])
            yield LATE
            for i in range(nt):
                w.norm_done = put(DVE, "beta", lambda e, i=i: e.scalar_tensor_tensor(
                    out=buf_b[:, i, :], in0=buf_b[:, i, :], scalar=w.rstd[:, 1, i:i + 1], in1=beta[:, :],
                    op0=ALU.mult, op1=ALU.add), z, root)
            z = w.norm_done
            w.norm_busy = False
            for pair in range(nt // 2):
                x3 = pair_op(pair, "x3", buf_b, buf_b, buf_a, ALU.add, z)
                if pair < nt // 2 - 1:
                    yield LATE
            w.free["a"] = x3
            w.free["b"] = put(SP, f"store{w.name}", lambda e: e.dma_start(
                out[rows, :].rearrange("(i p) d -> p i d", p=P), buf_b[:, :, :]), x3, dma=True)
            stores.append(w.free["b"])

        def run(generator):
            for _ in generator:
                pass

        load("wo", wo[:, :, :], ins["o_wT"].rearrange("(j p) n -> p j n", p=P))
        first, second = prep(0), prep(1)
        for generator, pieces in ((first, 4), (second, 2)):
            for _ in range(pieces):
                next(generator)
        filled = fill_padding()
        run(first)
        split_weights("k", wk_hl, H * HD)
        next(second)
        q_scaled, q_weights = scale_q()
        run(second)
        split_weights("q", wq_hl, 0, q_weights)
        for c in range(PER_BATCH):
            run(project_k(0, 0, c))
        split_weights("v", wv_hl, (H + KV) * HD)

        def setup_tail():
            nonlocal k2_ready, v2_ready, mask_ready, bq2_ready, route_w_ready, temp_ready
            load("wq2", wq2[:, :, :], ins["Wq"].rearrange("(c p) n -> p c n", p=P))
            load("wout2", wout2[:, :, :], ins["Wout"].rearrange("(c p) n -> p c n", p=P))
            wkv = buf_a[:, :, :].rearrange("p a b -> p (a b)").rearrange("p (c n) -> p c n", c=KC)
            load("wkv", wkv, ins["Wkv"].rearrange("(c p) n -> p c n", p=P), x_read[1])
            ctxT = buf_b[:, 0:2, :]
            load("ctxT", ctxT, ins["ctxT"].rearrange("(c p) n -> p c n", p=P))
            mask_words = buf_b[:, 3, HD:2 * HD].bitcast(mybir.dt.uint32)
            mask_u8 = buf_b[:, 3, HD:2 * HD].bitcast(U8)
            load("mask", mask_words, ins["mask"].broadcast_to([P, B * SC // 4]), q_scaled)
            load("sig", buf_c[:, :, 0:TILES], ins["sigT"].rearrange("(c p) n -> p c n", p=P), q_scaled)
            load("cw1", cw1[:, :, :], ins["cw1"].rearrange("(c p) n -> p c n", p=P))
            load("cw2", cw2[:, :], ins["cw2"])
            pad = fill(table[:, :], 0.0)
            parts = (("sw1", 0, 2 * GRID), ("sb1", 2 * GRID, GRID), ("sw2", 3 * GRID, GRID), ("sb2", 4 * GRID, 1),
                     ("directions", SMALL, D))
            for name, at, n in parts:
                table_ready.append(load(name, table[:, at:at + n], ins[name], pad))
            yield LATE
            yield LATE
            bq2_ready = put(DVE, "setup_v", lambda e: e.tensor_scalar(
                bq2[:, :], bq2[:, :], XHD ** -0.5, None, ALU.mult), loads["columns"])
            m = put(DVE, "setup_v", lambda e: e.tensor_copy(mask_add[:, :], mask_u8), loads["mask"])
            mask_ready = put(DVE, "setup_v", lambda e: e.tensor_scalar(
                mask_add[:, :], mask_add[:, :], -3e38, 3.0, ALU.mult, ALU.mult), m)
            yield EARLY
            for m_ in range(KC):
                at, ps, free = misc.take()
                for c in range(KC):
                    done = put(PE, "k2" if c else None, lambda e, m=m_, c=c, ps=ps: e.matmul(
                        ps[:, 0:B * SC], wkv[:, c, m * P:(m + 1) * P], ctxT[:, c, :], start=c == 0, stop=c == 1),
                        *free, loads["wkv"], loads["ctxT"])
                yield LATE
                k2_ready = put(ACTE, "k2T", lambda e, m=m_, ps=ps: e.activation(
                    k2T[:, m, :], ps[:, 0:B * SC], ACT.Identity, bias=bk2[:, m:m + 1]), done, loads["columns"])
                misc.free(at, k2_ready)
                yield EARLY
            for b in range(B):
                at, ps, free = misc.take()
                for hh in range(2):
                    for c in range(KC):
                        done = put(PE, "v2" if c else None, lambda e, b=b, c=c, hh=hh, ps=ps: e.matmul(
                            ps[hh * SC:(hh + 1) * SC, 0:D], ctxT[:, c, b * SC:(b + 1) * SC],
                            wkv[:, c, D:2 * D], start=c == 0, stop=c == 1), *free)
                main.free["a"] = done
                yield LATE
                for hh in range(2):
                    r = slice(hh * SC, (hh + 1) * SC)
                    v2_ready = put(DVE, "v2_block", lambda e, b=b, hh=hh, r=r, ps=ps: e.tensor_tensor(
                        v2_block[r, b, :, hh, :], ps[r, 0:D].rearrange("p (j a n) -> p j a n", a=2, n=XHD)[:, :, hh, :],
                        bv2[r, :].rearrange("p (j a n) -> p j a n", a=2, n=XHD)[:, :, hh, :], ALU.add),
                        done, loads["setup_rows"], filled)
                misc.free(at, v2_ready)
                yield EARLY if b < B - 1 else LATE
            raw = buf_c[:, :, 0:TILES]
            tern, diff = buf_c[:, :, TILES:2 * TILES], buf_c[:, :, 2 * TILES:3 * TILES]
            g = put(DVE, "sigs", lambda e: e.tensor_scalar(diff, raw, -0.3, None, ALU.is_lt), loads["sig"])
            g2 = put(DVE, "sigs", lambda e: e.tensor_scalar(tern, raw, 0.3, None, ALU.is_gt), loads["sig"])
            g = put(DVE, "sigs", lambda e: e.tensor_tensor(tern, tern, diff, ALU.subtract), g2)
            g = put(DVE, "sigs", lambda e: e.tensor_tensor(diff, tern, raw, ALU.subtract), g)
            sig = route_w[:, :, CL:]
            g = put(DVE, "sigs", lambda e: e.tensor_tensor(sig, raw, diff, ALU.add), g)
            by_tile = sig.rearrange("p k (c t) -> p k t c", c=CL)
            total, negative = buf_c[:, :, 192:192 + CL], buf_c[:, :, 208:208 + CL]
            g = put(DVE, "sigs", lambda e: e.tensor_tensor(total, by_tile[:, :, 0, :], by_tile[:, :, 1, :], ALU.add), g)
            for i in range(2, TPC):
                g = put(DVE, "sigs", lambda e, i=i: e.tensor_tensor(total, total, by_tile[:, :, i, :], ALU.add), g)
            yield LATE
            g = put(DVE, "sigs", lambda e: e.tensor_scalar(negative, total, 0.0, None, ALU.is_lt), g)
            g = put(DVE, "sigs", lambda e: e.tensor_scalar(total, total, 0.0, None, ALU.is_gt), g)
            route_w_ready = put(DVE, "sigs", lambda e: e.tensor_tensor(
                route_w[:, :, 0:CL], total, negative, ALU.subtract), g)
            main.free["c"] = [route_w_ready]
            g = put(DVE, "setup_v", lambda e: e.tensor_scalar(inv_temp[:, :], temperature, 1e-6, None, ALU.add), loads["rows"])
            g = put(DVE, "setup_v", lambda e: e.reciprocal(mag[:, 0:1], inv_temp[:, :]), g)
            g = put(DVE, "setup_v", lambda e: e.tensor_scalar(inv_temp[:, :], mag[:, 0:1], -1.0, None, ALU.mult), g)
            temp_ready = put(DVE, "setup_v", lambda e: e.tensor_tensor(
                knot_step[:, :], knots[:, 1:KNOTS], knots[:, 0:KNOTS - 1], ALU.subtract), g, loads["rows"])

        k2_ready = v2_ready = mask_ready = bq2_ready = route_w_ready = temp_ready = None
        table_ready = []

        Q_AHEAD, MAX_AHEAD, SHIFT_AHEAD, PV_BEHIND, FINISH_BEHIND = 14, 11, 4, 2, 4
        background = []
        HALF_AHEAD = 5
        extra = {}

        def at_step(step, piece):
            extra.setdefault(step, []).append(piece)

        period = PAIRS * KT
        for what, half, first in (("v", 0, 0), ("k", 1, 4), ("v", 1, 8)):
            for c in range(PER_BATCH):
                at_step(first + c, (what, 0, half, c))
        at_step(-Q_AHEAD, ("setup",))
        for b in range(B):
            start = b * PER_BATCH * period
            if b + 1 < B:
                at_step(start + 2 * KT, ("prep", 2 * b + 2))
                at_step(start + 6 * KT, ("prep", 2 * b + 3))
                last = start + (PER_BATCH - 1) * period
                for half in range(2):
                    for c in range(PER_BATCH):
                        at_step(last + (4 * half + 4) * KT + 1 + 2 * c, ("k", b + 1, half, c))
                        at_step(last + (4 * half + 5) * KT + 2 + 2 * c, ("v", b + 1, half, c))
        for t in range(CHUNKS - 1):
            at_step((t + 1) * period + FINISH_BEHIND + 1, ("tail", t))

        units, preps = [], []
        wanted = {}

        def go_on(generators, at, phase):
            if at >= len(generators) or wanted.get(generators[at], EARLY) != phase:
                return False
            wanted[generators[at]] = next(generators[at], None)
            return True

        for step in range(-Q_AHEAD, UNITS * KT + FINISH_BEHIND + 2):
            def unit_at(offset):
                u, r = divmod(step + offset, KT)
                return (u, r) if 0 <= u < UNITS else (None, r)

            u, r = unit_at(Q_AHEAD)
            if u is not None and r == 0:
                units.append(project_q(u))
            u, r = unit_at(SHIFT_AHEAD)
            if u is not None and r == 0:
                units.append(shift_rows(u))
            u, r = unit_at(-(KT - 1) - FINISH_BEHIND)
            if u is not None and r == 0:
                units.append(finish(u))
            for what, *rest in extra.get(step, []):
                if what in ("tail", "setup"):
                    background.append(tail(*rest, main) if rest else setup_tail())
                else:
                    preps.append({"k": project_k, "v": project_v, "prep": prep}[what](*rest))

            u, i = unit_at(MAX_AHEAD)
            if u is not None:
                take_max(u, i)
            crowded = any([go_on(units, at, EARLY) for at in range(len(units))])
            if not go_on(preps, 0, EARLY) and not go_on(background, 0, EARLY) and not crowded:
                go_on(background, 0, ALONE)
            u, kt = unit_at(-PV_BEHIND)
            if u is not None:
                attend(u, kt)
            for at in range(len(units)):
                go_on(units, at, LATE)
            go_on(preps, 0, LATE)
            go_on(background, 0, LATE)
            u, kt = unit_at(0)
            if u is not None:
                score_keys(u, kt)
            for generators in (units, preps, background):
                generators[:] = [g for g in generators if wanted.get(g, EARLY) is not None]
        for generators in (preps, background):
            for generator in generators:
                run(generator)

        for ring in (key_scores, max_scores):
            misc.buffers += ring.buffers
            misc.readers += ring.readers
        def flat(buffer):
            words = int(np.prod(buffer.shape[1:]))
            return [buffer[:, :] if len(buffer.shape) == 2 else
                    buffer[:, :, :].rearrange("p a b -> p (a b)"), words]

        regions = [flat(buffer) for buffer in (
            main.a, main.b, main.c, main.d, main.p2T, x_in, v_all, *main.weights.buffers, *probs.buffers)]

        def carve(name, shape):
            words = int(np.prod(shape[1:]))
            region = min((r for r in regions if r[1] >= words), key=lambda r: r[1])
            region[1] -= words
            view = region[0][:, region[1]:region[1] + words]
            if len(shape) == 2:
                return view
            letters = "abc"[:len(shape) - 1]
            return view.rearrange(f"p ({' '.join(letters)}) -> p {' '.join(letters)}",
                                  **dict(zip(letters, shape[1:])))

        halves = []
        for name, first in (("_first", 0), ("_second", NT // 2)):
            w = Workspace(name, NT // 2, first, carve)
            w.free["a"], w.free["b"] = sum_done[UNITS - 1], main.free["b"]
            halves.append(tail(CHUNKS - 1, w))
        for _ in range(HALF_AHEAD):
            next(halves[0])
        while halves:
            halves = [half for half in halves if next(half, None) is not None]

        block = ctx.enter_context(nc.Block())

        @block.tensor
        def _(eng):
            q.play(PE, eng)

        @block.scalar
        def _(eng):
            q.play(ACTE, eng)

        @block.vector
        def _(eng):
            q.play(DVE, eng)

        @block.gpsimd
        def _(eng):
            q.play(POOL, eng)

        @block.sync
        def _(eng):
            q.play(SP, eng)
            for name, value in stores[-3:]:
                eng.wait_ge(q.semaphores[name], value)


def kernel(**inputs):
    import numpy as np
    import concourse.bacc as bacc
    from concourse.bass_utils import run_bass_kernel_spmd

    a = {k: np.asarray(v) for k, v in inputs.items()}
    consts = np.zeros((P, P + 16 + HB), np.float32)
    consts[:, 0:P] = np.eye(P)
    consts[:, P:P + 8] = [-1, 1, 2, 3, 4, 5, 6, 100]
    consts[:, P + 8:P + 16] = np.arange(8, 0, -1)
    consts[np.arange(P), P + 16 + np.arange(P) // XHD] = 1
    qkv_b = a["L0_attn_qkv_b"]
    arrays = {
        "x": a["x"].reshape(B * S, D),
        "ctxT": a["ctx_1024"].reshape(B * SC, D).T,
        "mask": a["mask_BxS2_bf0"].reshape(1, B * SC).view(np.uint32),
        "columns": np.concatenate([
            qkv_b[0:H * HD].reshape(PAIRS, P).T, qkv_b[H * HD:(H + KV) * HD].reshape(KV // 2, P).T,
            a["L0_xattn_bq"].reshape(KC, P).T, a["L0_xattn_bkv"][0:D].reshape(KC, P).T,
            np.tile(a["L0_attn_scaling"], 2).reshape(P, 1), np.tile(a["L0_ffn_compress_b1"], 2).reshape(P, 1)], axis=1),
        "rows": np.concatenate([
            qkv_b[(H + KV) * HD:], a["L0_attn_o_b"], a["L0_xattn_bout"], a["L0_ffn_norm_gamma"],
            a["L0_ffn_norm_beta"], a["L0_ffn_compress_b2"], a["L0_ffn_knot_values"], a["L0_ffn_temperature"],
            a["L0_ffn_output_scale"]]).reshape(1, ROWS_N),
        "setup_rows": np.concatenate([a["L0_xattn_bkv"][D:], a["L0_attn_scaling"]]).reshape(1, D + HD),
        "qkv_wT": a["L0_attn_qkv_w"].T,
        "o_wT": a["L0_attn_o_w"].T,
        "Wq": a["L0_xattn_Wq"],
        "Wkv": a["L0_xattn_Wkv"],
        "Wout": a["L0_xattn_Wout"],
        "sigT": a["L0_ffn_signatures_raw"].T,
        "cw1": a["L0_ffn_compress_w1"],
        "cw2": a["L0_ffn_compress_w2"],
        "sw1": a["L0_ffn_spline_w1"].reshape(TILES, 2 * GRID),
        "sb1": a["L0_ffn_spline_b1"],
        "sw2": a["L0_ffn_spline_w2"].reshape(TILES, GRID),
        "sb2": a["L0_ffn_spline_b2"],
        "directions": a["L0_ffn_directions"],
        "consts": consts,
    }
    nc = bacc.Bacc("TRN2", target_bir_lowering=False, num_devices=1)
    in_map, ins = {}, {}
    for name, shape in INPUTS:
        array = np.ascontiguousarray(arrays[name])
        assert array.shape == shape, (name, array.shape)
        in_map[f"in_{name}"] = array
        ins[name] = nc.dram_tensor(f"in_{name}", shape, mybir.dt.from_np(array.dtype), kind="ExternalInput").ap()
    out = nc.dram_tensor("out_x", (B * S, D), F32, kind="ExternalOutput").ap()
    build(nc, ins, out)
    r = run_bass_kernel_spmd(nc, [in_map], core_ids=[0])
    return r.results[0]["out_x"].reshape(B, S, D)
```
